# Optimizing a Trainium2 kernel written in Bass

```python
import numpy as np
import jax
import jax.numpy as jnp

def _softmax(x, axis=-1):
    return jax.nn.softmax(x, axis=axis)
def _gelu(x):
    return jax.nn.gelu(x, approximate=True)
def _silu(x):
    return jax.nn.silu(x)
def _sigmoid(x):
    return jax.nn.sigmoid(x)
def _layernorm(x, axis=-1, eps=1e-5):
    m = jnp.mean(x, axis=axis, keepdims=True)
    v = jnp.var(x, axis=axis, keepdims=True)
    return (x - m) / jnp.sqrt(v + eps)
def _scatter_add(tgt, idx, src, axis=0):
    return tgt.at[idx].add(src)
def _segment_sum(src, seg, n):
    return jax.ops.segment_sum(src, seg, n)

kernel_name = 'mk_conv_seq_d2_conv_nchw512_3c52a3'

def setup_inputs(seed: int = 0):
    np.random.seed(seed)
    _w = jnp.asarray
    def _rec_inputs():
        import jax
        import jax.numpy as jnp
        _gk = jax.random.key(seed)
        x = -0.0002928 + 1 * jax.random.normal(jax.random.fold_in(_gk, 1), (8, 512, 32, 32), jnp.float32)
        return x
    x = _rec_inputs()
    def _L0_conv_setup():
        import jax, jax.numpy as jnp
        import numpy as np
        GROUPS = 32

        def group_norm(x, scale, bias, groups=GROUPS, eps=1e-05):
            B, C, H, W = x.shape
            xf = x.astype(jnp.float32).reshape(B, groups, C // groups, H, W)
            mean = xf.mean(axis=(2, 3, 4), keepdims=True)
            var = xf.var(axis=(2, 3, 4), keepdims=True)
            xf = (xf - mean) * jax.lax.rsqrt(var + eps)
            xf = xf.reshape(B, C, H, W)
            return (xf * scale[None, :, None, None] + bias[None, :, None, None]).astype(x.dtype)
        key = jax.random.key(seed)
        ks = jax.random.split(key, 7)
        B, C, H, W = (8, 512, 32, 32)
        x = jax.random.normal(ks[0], (B, C, H, W), dtype=jnp.float32)
        gn_scale = jnp.ones((C,), jnp.float32)
        gn_bias = jnp.zeros((C,), jnp.float32)
        qkv_w = jax.random.normal(ks[1], (3 * C, C), jnp.float32) * (1.0 / np.sqrt(C))
        qkv_b = jnp.zeros((3 * C,), jnp.float32)
        proj_w = jax.random.normal(ks[2], (C, C), jnp.float32) * (1.0 / np.sqrt(C))
        proj_b = jnp.zeros((C,), jnp.float32)
        return {'x': x, 'gn_scale': gn_scale, 'gn_bias': gn_bias, 'qkv_w': qkv_w, 'qkv_b': qkv_b, 'proj_w': proj_w, 'proj_b': proj_b}
    _L0_conv_all = _L0_conv_setup()
    _L0_conv_in = {k: v for k, v in _L0_conv_all.items() if k in ('gn_scale', 'gn_bias', 'qkv_w', 'qkv_b', 'proj_w', 'proj_b', )}
    del _L0_conv_all

    def _L1_conv_setup():
        import jax, jax.numpy as jnp
        import numpy as np
        B, C, H, W = (2, 512, 64, 64)
        DQK = C // 8
        key = jax.random.key(seed)
        ks = jax.random.split(key, 8)
        s = 0.05
        return {'x': jax.random.normal(ks[0], (B, C, H, W), jnp.float32), 'Wq': jax.random.normal(ks[1], (DQK, C), jnp.float32) * s, 'bq': jax.random.normal(ks[2], (DQK,), jnp.float32) * s, 'Wk': jax.random.normal(ks[3], (DQK, C), jnp.float32) * s, 'bk': jax.random.normal(ks[4], (DQK,), jnp.float32) * s, 'Wv': jax.random.normal(ks[5], (C, C), jnp.float32) * s, 'bv': jax.random.normal(ks[6], (C,), jnp.float32) * s, 'gamma': jax.random.normal(ks[7], (1,), jnp.float32)}
    _L1_conv_all = _L1_conv_setup()
    _L1_conv_in = {k: v for k, v in _L1_conv_all.items() if k in ('Wq', 'bq', 'Wk', 'bk', 'Wv', 'bv', 'gamma', )}
    del _L1_conv_all

    return {
        "x": x,
        "L0_conv_gn_scale": _L0_conv_in["gn_scale"],
        "L0_conv_gn_bias": _L0_conv_in["gn_bias"],
        "L0_conv_qkv_w": _L0_conv_in["qkv_w"],
        "L0_conv_qkv_b": _L0_conv_in["qkv_b"],
        "L0_conv_proj_w": _L0_conv_in["proj_w"],
        "L0_conv_proj_b": _L0_conv_in["proj_b"],
        "L1_conv_Wq": _L1_conv_in["Wq"],
        "L1_conv_bq": _L1_conv_in["bq"],
        "L1_conv_Wk": _L1_conv_in["Wk"],
        "L1_conv_bk": _L1_conv_in["bk"],
        "L1_conv_Wv": _L1_conv_in["Wv"],
        "L1_conv_bv": _L1_conv_in["bv"],
        "L1_conv_gamma": _L1_conv_in["gamma"],
    }

def reference(x, L0_conv_gn_scale, L0_conv_gn_bias, L0_conv_qkv_w, L0_conv_qkv_b, L0_conv_proj_w, L0_conv_proj_b, L1_conv_Wq, L1_conv_bq, L1_conv_Wk, L1_conv_bk, L1_conv_Wv, L1_conv_bv, L1_conv_gamma):
    import jax
    import jax.numpy as jnp
    def _L0_conv_ref(x, gn_scale, gn_bias, qkv_w, qkv_b, proj_w, proj_b):
        import jax, jax.numpy as jnp
        import numpy as np
        GROUPS = 32

        def group_norm(x, scale, bias, groups=GROUPS, eps=1e-05):
            B, C, H, W = x.shape
            xf = x.astype(jnp.float32).reshape(B, groups, C // groups, H, W)
            mean = xf.mean(axis=(2, 3, 4), keepdims=True)
            var = xf.var(axis=(2, 3, 4), keepdims=True)
            xf = (xf - mean) * jax.lax.rsqrt(var + eps)
            xf = xf.reshape(B, C, H, W)
            return (xf * scale[None, :, None, None] + bias[None, :, None, None]).astype(x.dtype)
        B, C, H, W = x.shape
        num_heads = 8
        head_dim = C // num_heads
        N = H * W
        h = group_norm(x, gn_scale, gn_bias)
        hf = h.reshape(B, C, N)
        qkv = jnp.einsum('oc,bcn->bon', qkv_w, hf) + qkv_b[None, :, None]
        q, k, v = jnp.split(qkv, 3, axis=1)
        q = q.reshape(B, num_heads, head_dim, N)
        k = k.reshape(B, num_heads, head_dim, N)
        v = v.reshape(B, num_heads, head_dim, N)
        scale = 1.0 / np.sqrt(head_dim).astype(np.float32)
        attn = jnp.einsum('bhcn,bhcm->bhnm', q * scale, k)
        attn = jax.nn.softmax(attn, axis=-1)
        out = jnp.einsum('bhnm,bhcm->bhcn', attn, v)
        out = out.reshape(B, C, N)
        out = jnp.einsum('oc,bcn->bon', proj_w, out) + proj_b[None, :, None]
        return x + out.reshape(B, C, H, W)

    def _L1_conv_ref(x, Wq, bq, Wk, bk, Wv, bv, gamma):
        import jax, jax.numpy as jnp
        import numpy as np
        B, C, H, W = (2, 512, 64, 64)
        DQK = C // 8
        b, c, h, w = x.shape
        n = h * w
        xf = x.reshape(b, c, n)
        q = jnp.einsum('dc,bcn->bnd', Wq, xf) + bq
        k = jnp.einsum('dc,bcn->bdn', Wk, xf) + bk[:, None]
        scores = jnp.einsum('bnd,bdm->bnm', q, k)
        atten = jax.nn.softmax(scores, axis=-1)
        v = jnp.einsum('dc,bcn->bdn', Wv, xf) + bv[:, None]
        res = jnp.einsum('bcj,bij->bci', v, atten)
        out = res.reshape(b, c, h, w) * gamma + x
        return out

    def _gn(v, G=32, eps=1e-5):
        B_, C_, H_, W_ = v.shape
        g = v.reshape(B_, G, C_ // G, H_, W_)
        m = jnp.mean(g, axis=(2, 3, 4), keepdims=True)
        s = jnp.var(g, axis=(2, 3, 4), keepdims=True)
        return ((g - m) / jnp.sqrt(s + eps)).reshape(v.shape)

    def _ln_c(v, eps=1e-6):
        m = jnp.mean(v, axis=1, keepdims=True)
        s = jnp.var(v, axis=1, keepdims=True)
        return (v - m) / jnp.sqrt(s + eps)

    def _ln_t(v, eps=1e-5):
        m = jnp.mean(v, axis=-1, keepdims=True)
        s = jnp.var(v, axis=-1, keepdims=True)
        return (v - m) / jnp.sqrt(s + eps)

    def _to_tokens(v):
        B_, C_, H_, W_ = v.shape
        return v.reshape(B_, C_, H_ * W_).transpose(0, 2, 1)
    def _from_tokens(t, like):
        B_, C_, H_, W_ = like.shape
        return t.transpose(0, 2, 1).reshape(B_, C_, H_, W_)

    x = _L0_conv_ref(x, L0_conv_gn_scale, L0_conv_gn_bias, L0_conv_qkv_w, L0_conv_qkv_b, L0_conv_proj_w, L0_conv_proj_b)
    x = _L1_conv_ref(x, L1_conv_Wq, L1_conv_bq, L1_conv_Wk, L1_conv_bk, L1_conv_Wv, L1_conv_bv, L1_conv_gamma)
    return x


_drawn_inputs = setup_inputs


def setup_inputs(seed=0):
    import zlib

    import numpy as np

    out = dict(_drawn_inputs(seed))
    spreads = {'L0_conv_gn_scale': (1.0, 0.2),
     'L0_conv_gn_bias': (0.0, 0.1),
     'L0_conv_qkv_b': (0.0, 0.1),
     'L0_conv_proj_b': (0.0, 0.1)}
    factors = {'L1_conv_bq': 7.372, 'L1_conv_bk': 8.0, 'L1_conv_bv': 8.0}
    for name, (base, spread) in spreads.items():
        noise = np.random.default_rng([zlib.crc32(name.encode()), seed]).standard_normal(out[name].shape)
        drawn = base * np.exp(spread * noise) if base else spread * noise
        out[name] = jnp.asarray(drawn.astype(out[name].dtype))
    for name, factor in factors.items():
        out[name] = (out[name] * factor).astype(out[name].dtype)
    return out
```

```python
from contextlib import ExitStack

import concourse.bass as bass
from concourse import mybir

F32 = mybir.dt.float32
F32R = mybir.dt.float32r
I32 = mybir.dt.int32
ALU = mybir.AluOpType
ACT = mybir.ActivationFunctionType
AX_X = mybir.AxisListType.X

P = 128
B, C, N = 8, 512, 1024
KC = C // P
BANK = 512
HALVES = N // BANK
HEADS, HD = 8, 64
PAIRS = HEADS // 2
QT = N // P
KT = N // P
UNIT = 4
UQ = UNIT * P // 2
GROUP = 16
DQK = 64
EPS = 1e-5
S_BANK, T_BANK, O_BANK = 0, 4, 6
QK_ITEMS = 2 * PAIRS * HALVES
V_ITEMS = N // P
PJ_ITEMS = KC * HALVES
STEPS = HEADS * QT
UNITS = STEPS // UNIT


def layer0(nc, x, w_qkv, w_proj, gn_scale, gn_bias, b_qk, b_v, b_proj, eye, x1_dram):
    q_dram = [nc.dram_tensor(f"q_{p}_scratch", (C, N), F32, kind="Internal").ap() for p in ("hi", "lo")]
    k_dram = [nc.dram_tensor(f"k_{p}_scratch", (C, N), F32, kind="Internal").ap() for p in ("hi", "lo")]
    v_dram = nc.dram_tensor("v_scratch", (HEADS, N, HD), F32, kind="Internal").ap()

    with ExitStack() as ctx:
        def sb(name, shape, dt=F32):
            return ctx.enter_context(nc.sbuf_tensor(name, shape, dt))

        def sem(name):
            return ctx.enter_context(nc.semaphore(name))

        ps = ctx.enter_context(nc.psum_tensor("ps0", [P, 8, BANK], F32))
        wq = [sb(f"wqkv_{p}", [P, KC, 3 * C], F32R) for p in ("hi", "lo")]
        wp = [sb(f"wproj_{p}", [P, KC, C], F32R) for p in ("hi", "lo")]
        ho = [sb(f"ho_{p}", [P, KC, N], F32R) for p in ("hi", "lo")]
        q_st = sb("q_st", [P, 2, N], F32R)
        k_hh = sb("k_hh", [P, 2, N], F32R)
        k_ll = sb("k_ll", [P, 2, N], F32R)
        v_sb = sb("v_sb", [P, 2, KT, HD])
        pt = sb("pt", [P, 2, KT, UNIT * P])
        pr = sb("pr", [P, 2, N])
        qk_stage = [sb(f"qk_stage_{p}", [P, 2, BANK], F32R) for p in ("hi", "lo")]
        f_stage = sb("f_stage", [P, 2, BANK])
        xb = sb("xb", [P, KC, N])
        xr = sb("xr", [P, 2, BANK])
        o_stage = sb("o_stage", [P, 2, 2, UQ], F32R)
        r_rep = sb("r_rep", [P, 2, P])
        r_bc = sb("r_bc", [P, 2, UQ])
        ident = sb("ident", [P, P])
        bv_row = sb("bv_row", [P, C])
        par = sb("par", [P, 8 + 3 * KC])
        neg_max = sb("neg_max", [P, 4])
        row_sum = sb("row_sum", [P, 2, UNIT])
        r_inv = sb("r_inv", [P, UNIT])
        bn6 = sb("bn6", [P, KC, 2, 6])
        st = sb("st", [P, 64])
        stt = sb("stt", [P, 64])
        sq = sb("sq", [P, 32])
        gs = sb("gs", [P, 10])
        gn = sb("gn", [P, 64])
        bqk_sb, scale_sb, bias_sb, bproj_sb = par[:, 0:8], par[:, 8:12], par[:, 12:16], par[:, 16:20]

        consts_in = sem("consts_in")
        w_in = sem("w_in")
        x_in = sem("x_in")
        w_hi_done = sem("w_hi_done")
        setup_done = sem("setup_done")
        gn_chain = sem("gn_chain")
        gn_done = sem("gn_done")
        h_hi_done = sem("h_hi_done")
        h_lo_done = sem("h_lo_done")
        qkv_ready = sem("qkv_ready")
        qk_hi_done = sem("qk_hi_done")
        qk_lo_done = sem("qk_lo_done")
        v_done = sem("v_done")
        qk_stored = [sem(f"qk_stored_{i}") for i in range(2)]
        v_stored = [sem(f"v_stored_{i}") for i in range(2)]
        qk_loaded = [sem(f"qk_loaded_{i}") for i in range(2)]
        v_loaded = [sem(f"v_loaded_{i}") for i in range(2)]
        s_ready = sem("s_ready")
        max_done = sem("max_done")
        exp_done = sem("exp_done")
        t_ready = sem("t_ready")
        t_act = sem("t_act")
        t_dve = sem("t_dve")
        inv_done = sem("inv_done")
        rep_done = sem("rep_done")
        pv_ready = sem("pv_ready")
        bc_done = sem("bc_done")
        o_chain = sem("o_chain")
        o_done = sem("o_done")
        o_moved = [sem(f"o_moved_{i}") for i in range(2)]
        xr_in = [sem(f"xr_in_{i}") for i in range(2)]
        pj_ready = sem("pj_ready")
        pj_done = sem("pj_done")
        x1_stored = [sem(f"x1_stored_{i}") for i in range(2)]

        def x_tiles(b):
            return x[b].rearrange("(k p) n -> p k n", p=P)

        def starts(b, pair):
            return b * STEPS + pair * 2 * QT, b * UNITS + pair * 4

        def over_pairs(eng, b, body):
            body(*starts(b, 0), None, 0, True, False)
            with eng.Fori(0, PAIRS - 2) as middle:
                body(*starts(b, middle + 1), b * UNITS + middle * 4 + 2, middle + 1, False, False)
            body(*starts(b, PAIRS - 1), b * UNITS + (PAIRS - 2) * 4 + 2, PAIRS - 1, False, True)

        with nc.Block() as block:

            @block.sync
            def _(sp):
                sp.dma_start(ident[:], eye).then_inc(consts_in, 16)
                sp.dma_start(bqk_sb, b_qk).then_inc(consts_in, 16)
                sp.dma_start(scale_sb, gn_scale).then_inc(consts_in, 16)
                sp.dma_start(bias_sb, gn_bias).then_inc(consts_in, 16)
                sp.dma_start(bproj_sb, b_proj).then_inc(consts_in, 16)
                sp.dma_start(bv_row[:], b_v.broadcast_to([P, C])).then_inc(consts_in, 16)
                sp.dma_start(xb[:], x_tiles(0)).then_inc(x_in, 16)
                sp.dma_start(pt[:].rearrange("p a k n -> p (a k n)")[:, 0:KC * 3 * C].rearrange("p (k o) -> p k o", k=KC),
                             w_qkv.rearrange("(k p) o -> p k o", p=P)).then_inc(w_in, 16)
                sp.dma_start(pt[:].rearrange("p a k n -> p (a k n)")[:, KC * 3 * C:KC * 4 * C].rearrange("p (k o) -> p k o", k=KC),
                             w_proj.rearrange("(k p) o -> p k o", p=P)).then_inc(w_in, 16)

                def load_stacks(rows, e):
                    lo, hi = slice(0, HD), slice(HD, P)
                    for dst, src in ((q_st[lo, e, :], q_dram[0]), (q_st[hi, e, :], q_dram[1]),
                                     (k_hh[lo, e, :], k_dram[0]), (k_hh[hi, e, :], k_dram[0]),
                                     (k_ll[lo, e, :], k_dram[1]), (k_ll[hi, e, :], k_dram[1])):
                        sp.dma_start(dst.bitcast(F32), src[rows, :]).then_inc(qk_loaded[e], 16)

                def load_v(head, e):
                    sp.dma_start(v_sb[:, e, :, :], v_dram[head].rearrange("(t p) d -> p t d", p=P)).then_inc(v_loaded[e], 16)

                with sp.Fori(0, B) as b:
                    for i in range(QK_ITEMS):
                        tile, half = i // 2, i % 2
                        pair, dst = tile // 2, (q_dram, k_dram)[tile % 2]
                        sp.wait_ge(qk_lo_done, b * QK_ITEMS + i + 1)
                        for part in range(2):
                            sp.dma_start(dst[part][pair * P:(pair + 1) * P, half * BANK:(half + 1) * BANK],
                                         qk_stage[part][:, i % 2, :].bitcast(F32)).then_inc(qk_stored[i % 2], 16)
                        if i == 5:
                            for slot in range(2):
                                sp.wait_ge(qk_stored[slot], b * 16 * QK_ITEMS + 64)
                            for e in range(2):
                                load_stacks(slice(e * HD, (e + 1) * HD), e)
                    sp.wait_ge(h_lo_done, b * KC + KC)
                    sp.dma_start(xb[:], x_tiles((b + 1) % B)).then_inc(x_in, 16)
                    for i in range(V_ITEMS):
                        sp.wait_ge(v_done, b * V_ITEMS + i + 1)
                        sp.dma_start(v_dram[:, i * P:(i + 1) * P, :].rearrange("h p d -> p h d"),
                                     f_stage[:, i % 2, :].rearrange("p (h d) -> p h d", h=HEADS)).then_inc(v_stored[i % 2], 16)
                    v_count = sp.to_reg(b * 8 * V_ITEMS + 8 * V_ITEMS)
                    qk_count = sp.to_reg(b * 16 * QK_ITEMS + 16 * QK_ITEMS)
                    for slot in range(2):
                        sp.wait_ge(v_stored[slot], v_count)
                        sp.wait_ge(qk_stored[slot], qk_count)
                    for e in range(2):
                        load_v(e, e)
                    with sp.Fori(0, PAIRS - 1) as pair:
                        for e in range(2):
                            head = pair * 2 + 2 + e
                            rows = bass.ds(head * HD, HD)
                            scores_of = sp.to_reg(b * STEPS + pair * 2 * QT + (e + 1) * QT)
                            values_of = sp.to_reg(b * UNITS + pair * 4 + (e + 1) * 2)
                            sp.wait_ge(s_ready, scores_of)
                            load_stacks(rows, e)
                            sp.wait_ge(pv_ready, values_of)
                            load_v(head, e)
                    for j in range(PJ_ITEMS):
                        o, half = j // 2, j % 2
                        if j >= 2:
                            sp.wait_ge(pj_done, b * PJ_ITEMS + j - 1)
                        sp.dma_start(xr[:, j % 2, :], x[b, o * P:(o + 1) * P, half * BANK:(half + 1) * BANK]
                                     ).then_inc(xr_in[j % 2], 16)

            @block.gpsimd
            def _(pool):
                def move_unit(u, slot, head_pair, e, half):
                    if slot is not None:
                        pool.wait_ge(o_done, u + 1)
                    for part in range(2):
                        for c in range(2):
                            dst = ho[part][e * HD:(e + 1) * HD, bass.ds(head_pair, 1),
                                           half * BANK + c * UQ:half * BANK + (c + 1) * UQ]
                            src = o_stage[c * HD:(c + 1) * HD, slot, part:part + 1, :]
                            pool.dma_start(dst.bitcast(F32), src.bitcast(F32)).then_inc(o_moved[slot], 16)

                with pool.Fori(0, B) as b:
                    with pool.Fori(0, PAIRS) as pair:
                        for k in range(4):
                            move_unit(b * UNITS + pair * 4 + k, k % 2, pair, k // 2, k % 2)
                    for j in range(PJ_ITEMS):
                        o, half = j // 2, j % 2
                        pool.wait_ge(pj_done, b * PJ_ITEMS + j + 1)
                        pool.dma_start(x1_dram[b, o * P:(o + 1) * P, half * BANK:(half + 1) * BANK],
                                       f_stage[:, j % 2, :]).then_inc(x1_stored[j % 2], 16)
                for slot in range(2):
                    pool.wait_ge(x1_stored[slot], B * PJ_ITEMS * 8)

            @block.scalar
            def _(act):
                raw = pt[:].rearrange("p a k n -> p (a k n)")
                act.wait_ge(w_in, 32)
                wraw = raw[:, 0:KC * 3 * C].rearrange("p (k o) -> p k o", k=KC)
                nc.scalar.activation(wq[0][:, :, 0:C], wraw[:, :, 0:C], ACT.Copy, scale=HD ** -0.5).then_inc(w_hi_done, 1)
                nc.scalar.activation(wq[0][:, :, C:3 * C], wraw[:, :, C:3 * C], ACT.Copy).then_inc(w_hi_done, 1)
                nc.scalar.activation(wp[0][:], raw[:, KC * 3 * C:KC * 4 * C].rearrange("p (k o) -> p k o", k=KC),
                                     ACT.Copy).then_inc(w_hi_done, 1)

                def exp(s, t, u_par):
                    act.wait_ge(max_done, s + 1)
                    nc.scalar.activation(pr[:, t % 2, :],
                                         ps[:, S_BANK + 2 * (t % 2):S_BANK + 2 * (t % 2) + 2, :].rearrange("p a n -> p (a n)"),
                                         ACT.Exp, bias=neg_max[:, t % 4:t % 4 + 1], scale=1.0,
                                         accum_out=row_sum[:, u_par, t % UNIT:t % UNIT + 1]).then_inc(exp_done, 1)

                def bc_copy(u, par):
                    act.wait_ge(pv_ready, u + 1)
                    nc.scalar.activation(r_bc[:, par, :], ps[:, O_BANK + par, UQ:2 * UQ], ACT.Copy).then_inc(bc_done, 1)

                def pair_steps(s0, u0, back, pair, first, last):
                    for i in range(2 * QT):
                        act.wait_ge(t_ready, 2 * s0 + 2 * i + 1)
                        nc.scalar.activation(pt[:, (i // UNIT) % 2, 0:4, (i % UNIT) * P:(i % UNIT + 1) * P],
                                             ps[:, T_BANK, :].rearrange("p (k q) -> p k q", k=4), ACT.Copy).then_inc(t_act, 1)
                        if i % UNIT == UNIT - 1 and not (first and i < UNIT):
                            bc_copy(u0 + i // UNIT - 1, (i // UNIT - 1) % 2)
                        if not (last and i == 2 * QT - 1):
                            exp(s0 + i + 1, (i + 1) % QT, ((i + 1) // UNIT) % 2)

                def split_hi(b):
                    for k in range(KC):
                        act.wait_ge(gn_done, b * KC + k + 1)
                        nc.scalar.activation(ho[0][:, k, :], xb[:, k, :], ACT.Identity, bias=bias_sb[:, k:k + 1],
                                             scale=1.0).then_inc(h_hi_done, 1)

                split_hi(0)
                with act.Fori(0, B) as b:
                    for i in range(QK_ITEMS):
                        tile = i // 2
                        col = (tile % 2) * 4 + tile // 2
                        act.wait_ge(qkv_ready, b * (QK_ITEMS + V_ITEMS) + i + 1)
                        if i >= 2:
                            act.wait_ge(qk_stored[i % 2], b * 16 * QK_ITEMS + (i // 2) * 32)
                        nc.scalar.activation(qk_stage[0][:, i % 2, :], ps[:, S_BANK + i % 4, :], ACT.Identity,
                                             bias=bqk_sb[:, col:col + 1], scale=1.0).then_inc(qk_hi_done, 1)
                    exp(b * STEPS, 0, 0)
                    over_pairs(act, b, pair_steps)
                    bc_copy(b * UNITS + UNITS - 1, 1)
                    act.wait_ge(pj_ready, b * PJ_ITEMS + PJ_ITEMS)
                    split_hi(b + 1)

            @block.vector
            def _(dve):
                raw = pt[:].rearrange("p a k n -> p (a k n)")
                wraw = raw[:, 0:KC * 3 * C].rearrange("p (k o) -> p k o", k=KC)
                dve.wait_ge(consts_in, 96)
                nc.vector.tensor_scalar(par[:, 0:4], par[:, 0:4], HD ** -0.5, None, ALU.mult).then_inc(setup_done, 1)
                dve.wait_ge(w_hi_done, 1)
                nc.vector.scalar_tensor_tensor(wq[1][:, :, 0:C], wraw[:, :, 0:C], HD ** -0.5, wq[0][:, :, 0:C].bitcast(F32),
                                               ALU.mult, ALU.subtract).then_inc(setup_done, 1)
                dve.wait_ge(w_hi_done, 2)
                nc.vector.tensor_tensor(wq[1][:, :, C:3 * C], wraw[:, :, C:3 * C], wq[0][:, :, C:3 * C].bitcast(F32),
                                        ALU.subtract).then_inc(setup_done, 1)
                dve.wait_ge(w_hi_done, 3)
                nc.vector.tensor_tensor(wp[1][:], raw[:, KC * 3 * C:KC * 4 * C].rearrange("p (k o) -> p k o", k=KC),
                                        wp[0][:].bitcast(F32), ALU.subtract).then_inc(setup_done, 1)
                dve.wait_ge(setup_done, 4)

                NEWTON = 4
                GN_LINKS = 16 + 3 * NEWTON

                def group_norm(b):
                    done = [0]

                    def link(ins):
                        done[0] += 1
                        ins.then_inc(gn_chain, 1)
                        dve.wait_ge(gn_chain, b * GN_LINKS + done[0])

                    dve.wait_ge(x_in, b * 16 + 16)
                    for k in range(KC):
                        for half in range(HALVES):
                            last = nc.vector.bn_stats(bn6[:, k, half, :], xb[:, k, half * BANK:(half + 1) * BANK])
                    link(last)
                    sv = st[:].rearrange("p (s c) -> p s c", s=2)
                    nc.vector.memset(sv[:, :, KC:32], 0.0)
                    for k in range(KC):
                        last = nc.vector.bn_aggr(sv[:, :, k], bn6[:, k, :, :].rearrange("p a s -> p (a s)"))
                    link(last)
                    link(nc.vector.transpose(stt[:], st[:]))
                    means = stt[:, 0:32].rearrange("p (g c) -> p g c", c=GROUP)
                    link(nc.vector.tensor_reduce(gs[:, 0:2], means, AX_X, ALU.add))
                    link(nc.vector.tensor_scalar(gs[:, 2:4], gs[:, 0:2], 1.0 / GROUP, None, ALU.mult))
                    group_mean = gs[:, 2:4].unsqueeze(2).broadcast_to([P, 2, GROUP])
                    sq3 = sq[:].rearrange("p (g c) -> p g c", c=GROUP)
                    link(nc.vector.tensor_tensor(sq3, means, group_mean, ALU.subtract))
                    link(nc.vector.tensor_tensor(sq[:], sq[:], sq[:], ALU.mult))
                    link(nc.vector.tensor_tensor(sq[:], sq[:], stt[:, 32:64], ALU.add))
                    link(nc.vector.tensor_reduce(gs[:, 4:6], sq3, AX_X, ALU.add))
                    link(nc.vector.tensor_scalar(gs[:, 4:6], gs[:, 4:6], 1.0 / GROUP, EPS, ALU.mult, ALU.add))
                    v, y, w = gs[:, 4:6], gs[:, 6:8], gs[:, 8:10]
                    link(nc.vector.tensor_scalar(y.bitcast(I32), v.bitcast(I32), 1, None, ALU.logical_shift_right))
                    link(nc.vector.tensor_scalar(y.bitcast(I32), y.bitcast(I32), -1.0, float(0x5f3759df), ALU.mult, ALU.add))
                    link(nc.vector.tensor_scalar(v, v, -0.5, None, ALU.mult))
                    for _ in range(NEWTON):
                        link(nc.vector.tensor_tensor(w, y, y, ALU.mult))
                        link(nc.vector.tensor_tensor(w, w, v, ALU.mult))
                        link(nc.vector.scalar_tensor_tensor(y, w, 1.5, y, ALU.add, ALU.mult))
                    nc.vector.tensor_copy(means, group_mean)
                    link(nc.vector.tensor_copy(stt[:, 32:64].rearrange("p (g c) -> p g c", c=GROUP),
                                               gs[:, 6:8].unsqueeze(2).broadcast_to([P, 2, GROUP])))
                    link(nc.vector.transpose(gn[:], stt[:]))
                    link(nc.vector.tensor_tensor(gn[:, 32:32 + KC], gn[:, 32:32 + KC], scale_sb, ALU.mult))
                    for k in range(KC):
                        nc.vector.tensor_scalar(xb[:, k, :], xb[:, k, :], gn[:, k:k + 1], gn[:, 32 + k:33 + k],
                                                ALU.subtract, ALU.mult).then_inc(gn_done, 1)
                    assert done[0] == GN_LINKS

                def row_max(s, t):
                    dve.wait_ge(s_ready, s + 1)
                    nc.vector.tensor_reduce(neg_max[:, t % 4:t % 4 + 1],
                                            ps[:, S_BANK + 2 * (t % 2):S_BANK + 2 * (t % 2) + 2, :].rearrange("p a n -> p (a n)"),
                                            AX_X, ALU.max, negate=True).then_inc(max_done, 1)

                def inverse_sums(s, u, par):
                    dve.wait_ge(exp_done, s + 1)
                    nc.vector.reciprocal(r_inv[:], row_sum[:, par, :]).then_inc(inv_done, 1)
                    dve.wait_ge(inv_done, u + 1)
                    rv = r_inv[:].rearrange("p (c j) -> p j c", c=2)
                    nc.vector.tensor_copy(r_rep[:].rearrange("p j (c d) -> p j c d", c=2),
                                          rv.unsqueeze(3).broadcast_to([P, 2, 2, HD])).then_inc(rep_done, 1)

                def unit_out(u, par, wait_stage, k_stage):
                    dve.wait_ge(bc_done, u + 1)
                    nc.vector.tensor_tensor(r_bc[:, par, :], ps[:, O_BANK + par, 0:UQ], r_bc[:, par, :], ALU.mult).then_inc(o_chain, 1)
                    if wait_stage:
                        dve.wait_ge(o_moved[par], k_stage)
                    dve.wait_ge(o_chain, 2 * u + 1)
                    nc.vector.tensor_copy(o_stage[:, par, 0, :], r_bc[:, par, :]).then_inc(o_chain, 1)
                    dve.wait_ge(o_chain, 2 * u + 2)
                    nc.vector.tensor_tensor(o_stage[:, par, 1, :], r_bc[:, par, :], o_stage[:, par, 0, :].bitcast(F32),
                                            ALU.subtract).then_inc(o_done, 1)

                def pair_steps(s0, u0, back, pair, first, last):
                    for i in range(2 * QT):
                        if not (last and i == 2 * QT - 1):
                            row_max(s0 + i + 1, (i + 1) % QT)
                        dve.wait_ge(t_ready, 2 * s0 + 2 * i + 2)
                        nc.vector.tensor_copy(pt[:, (i // UNIT) % 2, 4:8, (i % UNIT) * P:(i % UNIT + 1) * P],
                                              ps[:, T_BANK + 1, :].rearrange("p (k q) -> p k q", k=4)).then_inc(t_dve, 1)
                        if i % UNIT == UNIT - 1:
                            k = i // UNIT
                            inverse_sums(s0 + i, u0 + k, k % 2)
                            if not (first and k == 0):
                                former = k - 1 - (k - 1) % 2
                                unit_out(u0 + k - 1, (k - 1) % 2, not (first and k <= 2),
                                         (u0 + former if first else back + 2 + former) * 32)

                def split_lo(b):
                    for k in range(KC):
                        dve.wait_ge(h_hi_done, b * KC + k + 1)
                        nc.vector.scalar_tensor_tensor(ho[1][:, k, :], xb[:, k, :], bias_sb[:, k:k + 1], ho[0][:, k, :].bitcast(F32),
                                                       ALU.add, ALU.subtract).then_inc(h_lo_done, 1)

                group_norm(0)
                split_lo(0)
                with dve.Fori(0, B) as b:
                    for i in range(QK_ITEMS):
                        tile = i // 2
                        col = (tile % 2) * 4 + tile // 2
                        dve.wait_ge(qk_hi_done, b * QK_ITEMS + i + 1)
                        nc.vector.scalar_tensor_tensor(qk_stage[1][:, i % 2, :], ps[:, S_BANK + i % 4, :], bqk_sb[:, col:col + 1],
                                                       qk_stage[0][:, i % 2, :].bitcast(F32), ALU.add, ALU.subtract
                                                       ).then_inc(qk_lo_done, 1)
                    for i in range(V_ITEMS):
                        dve.wait_ge(qkv_ready, b * (QK_ITEMS + V_ITEMS) + QK_ITEMS + i + 1)
                        if i >= 2:
                            dve.wait_ge(v_stored[i % 2], b * V_ITEMS * 8 + (i // 2) * 16)
                        nc.vector.tensor_tensor(f_stage[:, i % 2, :], ps[:, S_BANK + i % 4, :], bv_row[:], ALU.add).then_inc(v_done, 1)
                    row_max(b * STEPS, 0)
                    over_pairs(dve, b, pair_steps)
                    unit_out(b * UNITS + UNITS - 1, 1, True, (b * UNITS + UNITS - 2) * 32)
                    group_norm(b + 1)
                    for slot in range(2):
                        dve.wait_ge(v_stored[slot], b * V_ITEMS * 8 + V_ITEMS * 8)
                    for j in range(PJ_ITEMS):
                        o = j // 2
                        dve.wait_ge(pj_ready, b * PJ_ITEMS + j + 1)
                        dve.wait_ge(xr_in[j % 2], b * PJ_ITEMS * 8 + (j // 2) * 16 + 16)
                        if j >= 2:
                            dve.wait_ge(x1_stored[j % 2], b * PJ_ITEMS * 8 + (j // 2) * 16)
                        nc.vector.scalar_tensor_tensor(f_stage[:, j % 2, :], ps[:, j, :], bproj_sb[:, o:o + 1], xr[:, j % 2, :],
                                                       ALU.add, ALU.add).then_inc(pj_done, 1)
                    split_lo(b + 1)
                    for slot in range(2):
                        dve.wait_ge(x1_stored[slot], b * PJ_ITEMS * 8 + PJ_ITEMS * 8)

            @block.tensor
            def _(pe):
                THREE = ((0, 0), (0, 1), (1, 0))

                def scores(s, e, t):
                    for half in range(HALVES):
                        for n, k_parts in enumerate((k_hh, k_ll)):
                            last = nc.tensor.matmul(ps[:, S_BANK + 2 * (t % 2) + half, :], q_st[:, e, t * P:(t + 1) * P],
                                                    k_parts[:, e, half * BANK:(half + 1) * BANK], start=(n == 0), stop=(n == 1))
                    last.then_inc(s_ready, 1)

                def transposes(t):
                    for j in range(2):
                        for k in range(4):
                            last = nc.tensor.transpose(ps[:, T_BANK + j, k * P:(k + 1) * P],
                                                       pr[:, t % 2, (4 * j + k) * P:(4 * j + k + 1) * P], ident[:])
                        last.then_inc(t_ready, 1)

                def sums_across(par):
                    for j in range(2):
                        nc.tensor.transpose(ps[:, O_BANK + par, UQ + j * P:UQ + (j + 1) * P], r_rep[:, j, :], ident[:])

                def values(par, e, k_tiles):
                    for k in k_tiles:
                        for c in range(2):
                            last = nc.tensor.matmul(ps[c * HD:(c + 1) * HD, O_BANK + par, 0:UQ], v_sb[:, e, k, :],
                                                    pt[:, par, k, c * UQ:(c + 1) * UQ], start=(k == 0), stop=(k == KT - 1))
                    if k_tiles[-1] == KT - 1:
                        last.then_inc(pv_ready, 1)

                def pair_steps(s0, u0, back, pair, first, last):
                    for i in range(2 * QT):
                        if not (last and i == 2 * QT - 1):
                            j = i + 1
                            if not (first and j == 1):
                                pe.wait_ge(exp_done, s0 + i)
                            if j % QT == 0:
                                e = (j // QT) % 2
                                h = pair * 2 + j // QT
                                pe.wait_ge(qk_loaded[e], head_loads(s0, j // QT) * 96)
                            scores(s0 + j, (j // QT) % 2, j % QT)
                        if not (first and i < UNIT):
                            k = i // UNIT - 1
                            if i % UNIT == 0:
                                pe.wait_ge(t_act, s0 + i)
                                pe.wait_ge(t_dve, s0 + i)
                                pe.wait_ge(rep_done, u0 + k + 1)
                                pe.wait_ge(v_loaded[(k // 2) % 2], head_loads(s0, k // 2) * 16)
                                if not (first and k < 2):
                                    pe.wait_ge(o_done, u0 + k - 1 if first else back + k + 1)
                                sums_across(k % 2)
                            values(k % 2, (k // 2) % 2, range(2 * (i % UNIT), 2 * (i % UNIT) + 2))
                        pe.wait_ge(exp_done, s0 + i + 1)
                        if not (first and i == 0):
                            pe.wait_ge(t_act, s0 + i)
                            pe.wait_ge(t_dve, s0 + i)
                        transposes(i % QT)

                def head_loads(s0, d):
                    return (s0 + 2 * QT * (d // 2)) // (2 * QT) + 1

                pe.wait_ge(setup_done, 4)
                with pe.Fori(0, B) as b:
                    pe.wait_ge(h_lo_done, b * KC + KC)
                    for i in range(QK_ITEMS):
                        tile, half = i // 2, i % 2
                        col = ((tile % 2) * 4 + tile // 2) * P
                        if i >= 4:
                            pe.wait_ge(qk_lo_done, b * QK_ITEMS + i - 3)
                        for k in range(KC):
                            for n, (w, h) in enumerate(THREE):
                                last = nc.tensor.matmul(ps[:, S_BANK + i % 4, :], wq[w][:, k, col:col + P],
                                                        ho[h][:, k, half * BANK:(half + 1) * BANK],
                                                        start=(k == 0 and n == 0), stop=(k == KC - 1 and n == 2))
                        last.then_inc(qkv_ready, 1)
                    for i in range(V_ITEMS):
                        if i < 4:
                            pe.wait_ge(qk_lo_done, b * QK_ITEMS + QK_ITEMS - 3 + i)
                        else:
                            pe.wait_ge(v_done, b * V_ITEMS + i - 3)
                        for k in range(KC):
                            for n, (h, w) in enumerate(THREE):
                                last = nc.tensor.matmul(ps[:, S_BANK + i % 4, :], ho[h][:, k, i * P:(i + 1) * P],
                                                        wq[w][:, k, 2 * C:3 * C],
                                                        start=(k == 0 and n == 0), stop=(k == KC - 1 and n == 2))
                        last.then_inc(qkv_ready, 1)
                    pe.wait_ge(qk_loaded[0], (b * PAIRS + 1) * 96)
                    pe.wait_ge(v_done, b * V_ITEMS + V_ITEMS)
                    scores(b * STEPS, 0, 0)
                    over_pairs(pe, b, pair_steps)
                    pe.wait_ge(t_act, b * STEPS + STEPS)
                    pe.wait_ge(t_dve, b * STEPS + STEPS)
                    pe.wait_ge(rep_done, b * UNITS + UNITS)
                    pe.wait_ge(o_done, b * UNITS + UNITS - 2)
                    sums_across(1)
                    values(1, 1, range(KT))
                    for group in range(2):
                        for part, ks in ((0, range(0, KC - 1)), (1, range(KC - 1, KC))):
                            for slot in range(2):
                                if group == 0:
                                    units = UNITS - 4 if part == 0 else UNITS
                                    pe.wait_ge(o_moved[slot], (b * UNITS + units) * 32)
                            for j in range(group * 4, group * 4 + 4):
                                o, half = j // 2, j % 2
                                if group == 1 and part == 0 and j == 6:
                                    pe.wait_ge(o_done, b * UNITS + UNITS)
                                for k in ks:
                                    for n, (w, h) in enumerate(THREE):
                                        last = nc.tensor.matmul(ps[:, j, :], wp[w][:, k, o * P:(o + 1) * P],
                                                                ho[h][:, k, half * BANK:(half + 1) * BANK],
                                                                start=(k == 0 and n == 0), stop=(k == KC - 1 and n == 2))
                                if part == 1:
                                    last.then_inc(pj_ready, 1)


def layer1(nc, x1_dram, w_qk, w_v, b_qk, b_v, gamma, eye, out):
    L1_STEPS, L1_UNITS = QT, QT // UNIT

    with ExitStack() as ctx:
        def sb(name, shape, dt=F32):
            return ctx.enter_context(nc.sbuf_tensor(name, shape, dt))

        def sem(name):
            return ctx.enter_context(nc.semaphore(name))

        ps = ctx.enter_context(nc.psum_tensor("ps1", [P, 8, BANK], F32))
        wqk = [sb(f"wqk_{p}", [P, KC, P], F32R) for p in ("hi", "lo")]
        wv = [sb(f"wv_{p}", [P, KC, C], F32R) for p in ("hi", "lo")]
        x_sb = sb("x_sb", [P, KC, N])
        xs = [sb(f"xs_{p}", [P, KC, N], F32R) for p in ("hi", "lo")]
        qk = [sb(f"qk_{p}", [P, N], F32R) for p in ("hi", "lo")]
        q_st = sb("l1_q_st", [P, N], F32R)
        k_hh = sb("l1_k_hh", [P, N], F32R)
        k_ll = sb("l1_k_ll", [P, N], F32R)
        vt = [sb(f"vt_{p}", [P, KT, C], F32R) for p in ("hi", "lo")]
        v_tmp = sb("v_tmp", [P, 3, BANK])
        pt = [sb(f"l1_pt_{p}", [P, KT, UNIT * P], F32R) for p in ("hi", "lo")]
        pr = sb("l1_pr", [P, 2, N])
        x_res = sb("x_res", [P, 2, BANK])
        o_sb = sb("o_sb", [P, 2, BANK])
        r_rep = sb("l1_r_rep", [P, UNIT, P])
        r_bc = sb("l1_r_bc", [P, BANK])
        ident = sb("l1_ident", [P, P])
        bv_row = sb("l1_bv_row", [P, C])
        par = sb("l1_par", [P, 2])
        neg_max = sb("l1_neg_max", [P, 4])
        row_sum = sb("l1_row_sum", [P, 2, UNIT])
        r_inv = sb("l1_r_inv", [P, UNIT])
        bqk_sb, gamma_sb = par[:, 0:1], par[:, 1:2]

        consts_in = sem("l1_consts_in")
        w_in = sem("l1_w_in")
        x_in = sem("l1_x_in")
        w_hi_done = sem("l1_w_hi_done")
        setup_done = sem("l1_setup_done")
        x_hi_done = sem("x_hi_done")
        x_lo_done = sem("x_lo_done")
        proj_ready = sem("proj_ready")
        qk_hi_done = sem("l1_qk_hi_done")
        qk_lo_done = sem("l1_qk_lo_done")
        stacked = sem("stacked")
        v_tmp_done = sem("v_tmp_done")
        v_hi_done = sem("v_hi_done")
        v_lo_done = sem("v_lo_done")
        s_ready = sem("l1_s_ready")
        max_done = sem("l1_max_done")
        exp_done = sem("l1_exp_done")
        t_ready = sem("l1_t_ready")
        t_hi = sem("t_hi")
        t_lo = sem("t_lo")
        inv_done = sem("l1_inv_done")
        rep_done = sem("l1_rep_done")
        bc_ready = sem("bc_ready")
        bc_done = sem("l1_bc_done")
        pv_ready = sem("l1_pv_ready")
        o_chain = sem("l1_o_chain")
        o_done = sem("l1_o_done")
        res_in = [sem(f"res_in_{i}") for i in range(2)]
        out_stored = [sem(f"out_stored_{i}") for i in range(2)]

        OUTS = L1_UNITS * KC

        def x_tiles(b):
            return x1_dram[b].rearrange("(k p) n -> p k n", p=P)

        with nc.Block() as block:

            @block.sync
            def _(sp):
                sp.dma_start(pt_raw_qk(pr), w_qk.rearrange("(k p) o -> p k o", p=P)).then_inc(w_in, 16)
                sp.dma_start(x_sb[:, :, 0:C], w_v.rearrange("(k p) o -> p k o", p=P)).then_inc(w_in, 16)
                sp.dma_start(ident[:], eye).then_inc(consts_in, 16)
                sp.dma_start(bqk_sb, b_qk).then_inc(consts_in, 16)
                sp.dma_start(gamma_sb, gamma.broadcast_to([P, 1])).then_inc(consts_in, 16)
                sp.dma_start(bv_row[:], b_v.broadcast_to([P, C])).then_inc(consts_in, 16)
                sp.wait_ge(setup_done, 2)
                sp.dma_start(x_sb[:], x_tiles(0)).then_inc(x_in, 16)
                with sp.Fori(0, B) as b:
                    sp.wait_ge(x_lo_done, b * KC + KC)
                    sp.dma_start(x_sb[:], x_tiles((b + 1) % B)).then_inc(x_in, 16)
                    sp.wait_ge(qk_lo_done, b * 2 + 2)
                    for dst, src in ((q_st[0:DQK, :], qk[0][0:DQK, :]), (q_st[DQK:P, :], qk[1][0:DQK, :]),
                                     (k_hh[0:DQK, :], qk[0][DQK:P, :]), (k_hh[DQK:P, :], qk[0][DQK:P, :]),
                                     (k_ll[0:DQK, :], qk[1][DQK:P, :]), (k_ll[DQK:P, :], qk[1][DQK:P, :])):
                        sp.dma_start(dst.bitcast(F32), src.bitcast(F32)).then_inc(stacked, 16)
                    for j in range(OUTS):
                        half, c = j // KC, j % KC
                        if j >= 2:
                            sp.wait_ge(o_done, b * OUTS + j - 1)
                        sp.dma_start(x_res[:, j % 2, :], x1_dram[b, c * P:(c + 1) * P, half * BANK:(half + 1) * BANK]
                                     ).then_inc(res_in[j % 2], 16)

            @block.gpsimd
            def _(pool):
                with pool.Fori(0, B) as b:
                    for j in range(OUTS):
                        half, c = j // KC, j % KC
                        pool.wait_ge(o_done, b * OUTS + j + 1)
                        pool.dma_start(out[b, c * P:(c + 1) * P, half * BANK:(half + 1) * BANK],
                                       o_sb[:, j % 2, :]).then_inc(out_stored[j % 2], 16)
                for slot in range(2):
                    pool.wait_ge(out_stored[slot], B * OUTS * 8)

            @block.scalar
            def _(act):
                act.wait_ge(w_in, 32)
                act.wait_ge(consts_in, 64)
                nc.scalar.activation(wqk[0][:], pt_raw_qk(pr), ACT.Copy).then_inc(w_hi_done, 1)
                nc.scalar.activation(wv[0][:], x_sb[:, :, 0:C], ACT.Copy).then_inc(w_hi_done, 1)

                def split_hi(b):
                    act.wait_ge(x_in, b * 16 + 16)
                    for k in range(KC):
                        nc.scalar.activation(xs[0][:, k, :], x_sb[:, k, :], ACT.Copy).then_inc(x_hi_done, 1)

                def exp(s, t):
                    act.wait_ge(max_done, s + 1)
                    nc.scalar.activation(pr[:, t % 2, :],
                                         ps[:, S_BANK + 2 * (t % 2):S_BANK + 2 * (t % 2) + 2, :].rearrange("p a n -> p (a n)"),
                                         ACT.Exp, bias=neg_max[:, t % 4:t % 4 + 1], scale=1.0,
                                         accum_out=row_sum[:, t // UNIT, t % UNIT:t % UNIT + 1]).then_inc(exp_done, 1)

                split_hi(0)
                with act.Fori(0, B) as b:
                    for half in range(HALVES):
                        act.wait_ge(proj_ready, b * (HALVES + V_ITEMS) + half + 1)
                        nc.scalar.activation(qk[0][:, half * BANK:(half + 1) * BANK], ps[:, half, :], ACT.Identity,
                                             bias=bqk_sb, scale=1.0).then_inc(qk_hi_done, 1)
                    for i in range(V_ITEMS):
                        act.wait_ge(v_tmp_done, b * V_ITEMS + i + 1)
                        nc.scalar.activation(vt[0][:, i, :], v_tmp[:, i % 3, :], ACT.Copy).then_inc(v_hi_done, 1)
                    exp(b * L1_STEPS, 0)
                    for i in range(L1_STEPS):
                        for j in range(2):
                            act.wait_ge(t_ready, b * 2 * L1_STEPS + 2 * i + j + 1)
                            nc.scalar.activation(pt[0][:, 4 * j:4 * j + 4, (i % UNIT) * P:(i % UNIT + 1) * P],
                                                 ps[:, T_BANK + j, :].rearrange("p (k q) -> p k q", k=4), ACT.Copy).then_inc(t_hi, 1)
                        if i % UNIT == UNIT - 1:
                            act.wait_ge(bc_ready, b * L1_UNITS + i // UNIT + 1)
                            nc.scalar.activation(r_bc[:], ps[:, O_BANK + i // UNIT, :], ACT.Copy).then_inc(bc_done, 1)
                        if i < L1_STEPS - 1:
                            exp(b * L1_STEPS + i + 1, i + 1)
                    split_hi(b + 1)

            @block.vector
            def _(dve):
                dve.wait_ge(consts_in, 64)
                dve.wait_ge(w_hi_done, 1)
                nc.vector.tensor_tensor(wqk[1][:], pt_raw_qk(pr), wqk[0][:].bitcast(F32), ALU.subtract).then_inc(setup_done, 1)
                dve.wait_ge(w_hi_done, 2)
                nc.vector.tensor_tensor(wv[1][:], x_sb[:, :, 0:C], wv[0][:].bitcast(F32), ALU.subtract).then_inc(setup_done, 1)

                def split_lo(b):
                    for k in range(KC):
                        dve.wait_ge(x_hi_done, b * KC + k + 1)
                        nc.vector.tensor_tensor(xs[1][:, k, :], x_sb[:, k, :], xs[0][:, k, :].bitcast(F32),
                                                ALU.subtract).then_inc(x_lo_done, 1)

                def row_max(s, t):
                    dve.wait_ge(s_ready, s + 1)
                    nc.vector.tensor_reduce(neg_max[:, t % 4:t % 4 + 1],
                                            ps[:, S_BANK + 2 * (t % 2):S_BANK + 2 * (t % 2) + 2, :].rearrange("p a n -> p (a n)"),
                                            AX_X, ALU.max, negate=True).then_inc(max_done, 1)

                split_lo(0)
                with dve.Fori(0, B) as b:
                    for half in range(HALVES):
                        dve.wait_ge(qk_hi_done, b * HALVES + half + 1)
                        nc.vector.scalar_tensor_tensor(qk[1][:, half * BANK:(half + 1) * BANK], ps[:, half, :], bqk_sb,
                                                       qk[0][:, half * BANK:(half + 1) * BANK].bitcast(F32),
                                                       ALU.add, ALU.subtract).then_inc(qk_lo_done, 1)
                    for i in range(V_ITEMS + 1):
                        if i < V_ITEMS:
                            dve.wait_ge(proj_ready, b * (HALVES + V_ITEMS) + HALVES + i + 1)
                            if i >= 3:
                                dve.wait_ge(v_lo_done, b * V_ITEMS + i - 2)
                            nc.vector.tensor_tensor(v_tmp[:, i % 3, :], ps[:, (HALVES + i) % 4, :], bv_row[:],
                                                    ALU.add).then_inc(v_tmp_done, 1)
                        if i > 0:
                            dve.wait_ge(v_hi_done, b * V_ITEMS + i)
                            nc.vector.tensor_tensor(vt[1][:, i - 1, :], v_tmp[:, (i - 1) % 3, :], vt[0][:, i - 1, :].bitcast(F32),
                                                    ALU.subtract).then_inc(v_lo_done, 1)
                    row_max(b * L1_STEPS, 0)
                    for i in range(L1_STEPS):
                        unit = i // UNIT
                        if i % UNIT != UNIT - 1:
                            row_max(b * L1_STEPS + i + 1, i + 1)
                        for j in range(2):
                            dve.wait_ge(t_hi, b * 2 * L1_STEPS + 2 * i + j + 1)
                            nc.vector.tensor_tensor(pt[1][:, 4 * j:4 * j + 4, (i % UNIT) * P:(i % UNIT + 1) * P],
                                                    ps[:, T_BANK + j, :].rearrange("p (k q) -> p k q", k=4),
                                                    pt[0][:, 4 * j:4 * j + 4, (i % UNIT) * P:(i % UNIT + 1) * P].bitcast(F32),
                                                    ALU.subtract).then_inc(t_lo, 1)
                        if i % UNIT == UNIT - 1:
                            dve.wait_ge(exp_done, b * L1_STEPS + i + 1)
                            nc.vector.reciprocal(r_inv[:], row_sum[:, unit, :]).then_inc(inv_done, 1)
                            dve.wait_ge(inv_done, b * L1_UNITS + unit + 1)
                            nc.vector.tensor_copy(r_rep[:], r_inv[:].unsqueeze(2).broadcast_to([P, UNIT, P])).then_inc(rep_done, 1)
                            if i < L1_STEPS - 1:
                                row_max(b * L1_STEPS + i + 1, i + 1)
                            else:
                                split_lo(b + 1)
                            dve.wait_ge(bc_done, b * L1_UNITS + unit + 1)
                            for c in range(KC):
                                j = unit * KC + c
                                dve.wait_ge(pv_ready, b * OUTS + j + 1)
                                if j >= 2:
                                    dve.wait_ge(out_stored[j % 2], b * OUTS * 8 + (j // 2) * 16)
                                nc.vector.tensor_tensor(o_sb[:, j % 2, :], ps[:, O_BANK + (unit + 1 + c) % 2, :], r_bc[:],
                                                        ALU.mult).then_inc(o_chain, 1)
                                dve.wait_ge(o_chain, b * OUTS + j + 1)
                                dve.wait_ge(res_in[j % 2], b * OUTS * 8 + (j // 2) * 16 + 16)
                                nc.vector.scalar_tensor_tensor(o_sb[:, j % 2, :], o_sb[:, j % 2, :], gamma_sb, x_res[:, j % 2, :],
                                                               ALU.mult, ALU.add).then_inc(o_done, 1)
                    for slot in range(2):
                        dve.wait_ge(out_stored[slot], b * OUTS * 8 + OUTS * 8)

            @block.tensor
            def _(pe):
                THREE = ((0, 0), (0, 1), (1, 0))

                def scores(t):
                    for half in range(HALVES):
                        for n, k_parts in enumerate((k_hh, k_ll)):
                            last = nc.tensor.matmul(ps[:, S_BANK + 2 * (t % 2) + half, :], q_st[:, t * P:(t + 1) * P],
                                                    k_parts[:, half * BANK:(half + 1) * BANK], start=(n == 0), stop=(n == 1))
                    last.then_inc(s_ready, 1)

                pe.wait_ge(setup_done, 2)
                with pe.Fori(0, B) as b:
                    pe.wait_ge(x_lo_done, b * KC + KC)
                    for half in range(HALVES):
                        for k in range(KC):
                            for n, (w, h) in enumerate(THREE):
                                last = nc.tensor.matmul(ps[:, half, :], wqk[w][:, k, :], xs[h][:, k, half * BANK:(half + 1) * BANK],
                                                        start=(k == 0 and n == 0), stop=(k == KC - 1 and n == 2))
                        last.then_inc(proj_ready, 1)
                    for i in range(V_ITEMS):
                        if 2 <= i < 4:
                            pe.wait_ge(qk_lo_done, b * HALVES + i - 1)
                        elif i >= 4:
                            pe.wait_ge(v_tmp_done, b * V_ITEMS + i - 3)
                        for k in range(KC):
                            for n, (h, w) in enumerate(THREE):
                                last = nc.tensor.matmul(ps[:, (HALVES + i) % 4, :], xs[h][:, k, i * P:(i + 1) * P], wv[w][:, k, :],
                                                        start=(k == 0 and n == 0), stop=(k == KC - 1 and n == 2))
                        last.then_inc(proj_ready, 1)
                    pe.wait_ge(stacked, b * 96 + 96)
                    pe.wait_ge(v_tmp_done, b * V_ITEMS + V_ITEMS)
                    scores(0)
                    for i in range(L1_STEPS):
                        unit = i // UNIT
                        if i < L1_STEPS - 1:
                            if i > 0:
                                pe.wait_ge(exp_done, b * L1_STEPS + i)
                            scores(i + 1)
                        pe.wait_ge(exp_done, b * L1_STEPS + i + 1)
                        for j in range(2):
                            if i > 0:
                                pe.wait_ge(t_lo, b * 2 * L1_STEPS + 2 * (i - 1) + j + 1)
                            for k in range(4):
                                last = nc.tensor.transpose(ps[:, T_BANK + j, k * P:(k + 1) * P],
                                                           pr[:, i % 2, (4 * j + k) * P:(4 * j + k + 1) * P], ident[:])
                            last.then_inc(t_ready, 1)
                        if i % UNIT == UNIT - 1:
                            pe.wait_ge(rep_done, b * L1_UNITS + unit + 1)
                            if unit == 1:
                                pe.wait_ge(o_done, b * OUTS + KC - 1)
                            for q in range(UNIT):
                                last = nc.tensor.transpose(ps[:, O_BANK + unit, q * P:(q + 1) * P], r_rep[:, q, :], ident[:])
                            last.then_inc(bc_ready, 1)
                            pe.wait_ge(t_lo, b * 2 * L1_STEPS + 2 * i + 2)
                            if unit == 0:
                                pe.wait_ge(v_lo_done, b * V_ITEMS + V_ITEMS)
                            for c in range(KC):
                                j = unit * KC + c
                                if j == 0:
                                    pass
                                elif c == 0:
                                    pe.wait_ge(o_done, b * OUTS + j)
                                elif c == 1:
                                    pe.wait_ge(bc_done, b * L1_UNITS + unit + 1)
                                else:
                                    pe.wait_ge(o_done, b * OUTS + j - 1)
                                for k in range(KT):
                                    for n, (v, p) in enumerate(THREE):
                                        last = nc.tensor.matmul(ps[:, O_BANK + (unit + 1 + c) % 2, :],
                                                                vt[v][:, k, c * P:(c + 1) * P], pt[p][:, k, :],
                                                                start=(k == 0 and n == 0), stop=(k == KT - 1 and n == 2))
                                last.then_inc(pv_ready, 1)


def pt_raw_qk(pr):
    return pr[:].rearrange("p a n -> p (a n)")[:, 0:KC * P].rearrange("p (k o) -> p k o", k=KC)


def build(nc, arrays):
    def dram_in(name):
        return nc.dram_tensor(name, arrays[name].shape, F32, kind="ExternalInput").ap()

    t = {name: dram_in(name) for name in arrays}
    out = nc.dram_tensor("out", (B, C, N), F32, kind="ExternalOutput").ap()
    x1 = nc.dram_tensor("x1_scratch", (B, C, N), F32, kind="Internal").ap()
    layer0(nc, t["x"], t["w_qkv"], t["w_proj"], t["gn_scale"], t["gn_bias"], t["b_qk"], t["b_v"], t["b_proj"], t["eye"], x1)
    layer1(nc, x1, t["w_qk1"], t["w_v1"], t["b_qk1"], t["b_v1"], t["gamma"], t["eye"], out)


def kernel(x, L0_conv_gn_scale, L0_conv_gn_bias, L0_conv_qkv_w, L0_conv_qkv_b, L0_conv_proj_w, L0_conv_proj_b,
           L1_conv_Wq, L1_conv_bq, L1_conv_Wk, L1_conv_bk, L1_conv_Wv, L1_conv_bv, L1_conv_gamma):
    import numpy as np
    import concourse.bacc as bacc
    from concourse.bass_utils import run_bass_kernel_spmd

    def cols(a):
        return np.ascontiguousarray(np.asarray(a).reshape(-1, P).T)

    qkv_b = np.asarray(L0_conv_qkv_b)
    arrays = {
        "x": np.ascontiguousarray(np.asarray(x).reshape(B, C, N)),
        "w_qkv": np.ascontiguousarray(np.asarray(L0_conv_qkv_w).T),
        "w_proj": np.ascontiguousarray(np.asarray(L0_conv_proj_w).T),
        "gn_scale": cols(L0_conv_gn_scale),
        "gn_bias": cols(L0_conv_gn_bias),
        "b_qk": cols(qkv_b[0:2 * C]),
        "b_v": np.ascontiguousarray(qkv_b[2 * C:3 * C].reshape(1, C)),
        "b_proj": cols(L0_conv_proj_b),
        "eye": np.eye(P, dtype=np.float32),
        "w_qk1": np.ascontiguousarray(np.concatenate([np.asarray(L1_conv_Wq), np.asarray(L1_conv_Wk)], axis=0).T),
        "w_v1": np.ascontiguousarray(np.asarray(L1_conv_Wv).T),
        "b_qk1": np.ascontiguousarray(np.concatenate([np.asarray(L1_conv_bq), np.asarray(L1_conv_bk)]).reshape(P, 1)),
        "b_v1": np.ascontiguousarray(np.asarray(L1_conv_bv).reshape(1, C)),
        "gamma": np.ascontiguousarray(np.asarray(L1_conv_gamma).reshape(1, 1)),
    }
    nc = bacc.Bacc("TRN2", target_bir_lowering=False, num_devices=1)
    build(nc, arrays)
    r = run_bass_kernel_spmd(nc, [arrays], core_ids=[0])
    return r.results[0]["out"].reshape(B, C, 32, 32)
```

```python
from contextlib import ExitStack

import concourse.bass as bass
from concourse import mybir

F32 = mybir.dt.float32
F32R = mybir.dt.float32r
I32 = mybir.dt.int32
ALU = mybir.AluOpType
ACT = mybir.ActivationFunctionType
AX_X = mybir.AxisListType.X

P = 128
B, C, N = 8, 512, 1024
KC = C // P
BANK = 512
HALVES = N // BANK
HEADS, HD = 8, 64
PAIRS = HEADS // 2
QT = N // P
KT = N // P
UNIT = 4
UQ = UNIT * P // 2
GROUP = 16
DQK = 64
EPS = 1e-5
S_BANK, T_BANK, O_BANK = 0, 4, 6
QK_ITEMS = 2 * PAIRS * HALVES
V_ITEMS = N // P
PJ_ITEMS = KC * HALVES
STEPS = HEADS * QT
UNITS = STEPS // UNIT


def layer0(nc, x, w_qkv, w_proj, gn_scale, gn_bias, b_qk, b_v, b_proj, eye, x1_dram):
    q_dram = [nc.dram_tensor(f"q_{p}_scratch", (C, N), F32, kind="Internal").ap() for p in ("hi", "lo")]
    k_dram = [nc.dram_tensor(f"k_{p}_scratch", (C, N), F32, kind="Internal").ap() for p in ("hi", "lo")]
    v_dram = nc.dram_tensor("v_scratch", (HEADS, N, HD), F32, kind="Internal").ap()

    with ExitStack() as ctx:
        def sb(name, shape, dt=F32):
            return ctx.enter_context(nc.sbuf_tensor(name, shape, dt))

        def sem(name):
            return ctx.enter_context(nc.semaphore(name))

        ps = ctx.enter_context(nc.psum_tensor("ps0", [P, 8, BANK], F32))
        wq = [sb(f"wqkv_{p}", [P, KC, 3 * C], F32R) for p in ("hi", "lo")]
        wp = [sb(f"wproj_{p}", [P, KC, C], F32R) for p in ("hi", "lo")]
        ho = [sb(f"ho_{p}", [P, KC, N], F32R) for p in ("hi", "lo")]
        q_st = sb("q_st", [P, 2, N], F32R)
        k_hh = sb("k_hh", [P, 2, N], F32R)
        k_ll = sb("k_ll", [P, 2, N], F32R)
        v_sb = sb("v_sb", [P, 2, KT, HD])
        pt = sb("pt", [P, 2, KT, UNIT * P])
        pr = sb("pr", [P, 2, N])
        qk_stage = [sb(f"qk_stage_{p}", [P, 2, BANK], F32R) for p in ("hi", "lo")]
        v_stage = sb("v_stage", [P, 2, BANK])
        xb = sb("xb", [P, KC, N])
        o_stage = sb("o_stage", [P, 2, 2, UQ], F32R)
        r_rep = sb("r_rep", [P, 2, P])
        r_bc = sb("r_bc", [P, 2, UQ])
        ident = sb("ident", [P, P])
        bv_row = sb("bv_row", [P, C])
        par = sb("par", [P, 8 + 3 * KC])
        neg_max = sb("neg_max", [P, 4])
        row_sum = sb("row_sum", [P, 2, UNIT])
        r_inv = sb("r_inv", [P, UNIT])
        bn6 = sb("bn6", [P, KC, 2, 6])
        st = sb("st", [P, 64])
        stt = sb("stt", [P, 64])
        sq = sb("sq", [P, 32])
        gs = sb("gs", [P, 10])
        gn = sb("gn", [P, 64])
        bqk_sb, scale_sb, bias_sb, bproj_sb = par[:, 0:8], par[:, 8:12], par[:, 12:16], par[:, 16:20]

        consts_in = sem("consts_in")
        w_in = [sem(f"w_in_{i}") for i in range(4)]
        x_in = sem("x_in")
        w_hi_done = sem("w_hi_done")
        w_lo_done = sem("w_lo_done")
        setup_done = sem("setup_done")
        gn_chain = sem("gn_chain")
        gn_done = sem("gn_done")
        h_hi_done = sem("h_hi_done")
        h_lo_done = sem("h_lo_done")
        qkv_ready = sem("qkv_ready")
        qk_hi_done = sem("qk_hi_done")
        qk_lo_done = sem("qk_lo_done")
        v_done = sem("v_done")
        qk_stored = [sem(f"qk_stored_{i}") for i in range(2)]
        v_stored = [sem(f"v_stored_{i}") for i in range(2)]
        qk_loaded = [sem(f"qk_loaded_{i}") for i in range(2)]
        v_loaded = [sem(f"v_loaded_{i}") for i in range(2)]
        s_ready = sem("s_ready")
        max_done = sem("max_done")
        exp_done = sem("exp_done")
        t_ready = sem("t_ready")
        t_act = sem("t_act")
        t_dve = sem("t_dve")
        inv_done = sem("inv_done")
        rep_done = sem("rep_done")
        pv_ready = sem("pv_ready")
        bc_done = sem("bc_done")
        o_chain = sem("o_chain")
        o_done = sem("o_done")
        o_moved = [sem(f"o_moved_{i}") for i in range(2)]
        xr_in = sem("xr_in")
        pj_read = sem("pj_read")
        pj_ready = sem("pj_ready")
        pj_done = sem("pj_done")
        x1_stored = sem("x1_stored")

        raw = pt[:].rearrange("p a k n -> p (a k n)")
        w_raw = [raw[:, i * KC * C:(i + 1) * KC * C].rearrange("p (k o) -> p k o", k=KC) for i in range(4)]
        w_parts = [[wq[part][:, :, i * C:(i + 1) * C] for i in range(3)] + [wp[part][:]] for part in range(2)]
        res = pt[:, 0, :, :].rearrange("p k n -> p (k n)").rearrange("p (j n) -> p j n", n=BANK)

        def x_tiles(b):
            return x[b].rearrange("(k p) n -> p k n", p=P)

        def starts(b, pair):
            return b * STEPS + pair * 2 * QT, b * UNITS + pair * 4

        def over_pairs(eng, b, body):
            body(*starts(b, 0), None, 0, True, False)
            with eng.Fori(0, PAIRS - 2) as middle:
                body(*starts(b, middle + 1), b * UNITS + middle * 4 + 2, middle + 1, False, False)
            body(*starts(b, PAIRS - 1), b * UNITS + (PAIRS - 2) * 4 + 2, PAIRS - 1, False, True)

        NEWTON = 4
        GN_LINKS = 16 + 3 * NEWTON

        with nc.Block() as block:

            @block.sync
            def _(sp):
                sp.dma_start(xb[:], x_tiles(0)).then_inc(x_in, 16)
                sp.dma_start(ident[:], eye).then_inc(consts_in, 16)
                sp.dma_start(bqk_sb, b_qk).then_inc(consts_in, 16)
                sp.dma_start(scale_sb, gn_scale).then_inc(consts_in, 16)
                sp.dma_start(bias_sb, gn_bias).then_inc(consts_in, 16)
                sp.dma_start(bproj_sb, b_proj).then_inc(consts_in, 16)
                sp.dma_start(bv_row[:], b_v.broadcast_to([P, C])).then_inc(consts_in, 16)
                for block_of in (2, 0, 1, 3):
                    src = w_proj if block_of == 3 else w_qkv[:, block_of * C:(block_of + 1) * C]
                    sp.dma_start(w_raw[block_of], src.rearrange("(k p) o -> p k o", p=P)).then_inc(w_in[block_of], 16)

                def load_stack(rows, e, n):
                    lo, hi = slice(0, HD), slice(HD, P)
                    dst, src = ((q_st[lo, e, :], q_dram[0]), (q_st[hi, e, :], q_dram[1]),
                                (k_hh[lo, e, :], k_dram[0]), (k_hh[hi, e, :], k_dram[0]),
                                (k_ll[lo, e, :], k_dram[1]), (k_ll[hi, e, :], k_dram[1]))[n]
                    sp.dma_start(dst.bitcast(F32), src[rows, :]).then_inc(qk_loaded[e], 16)

                def load_v(head, e):
                    sp.dma_start(v_sb[:, e, :, :], v_dram[head].rearrange("(t p) d -> p t d", p=P)).then_inc(v_loaded[e], 16)

                with sp.Fori(0, B) as b:
                    for i in range(V_ITEMS):
                        sp.wait_ge(v_done, b * V_ITEMS + i + 1)
                        sp.dma_start(v_dram[:, i * P:(i + 1) * P, :].rearrange("h p d -> p h d"),
                                     v_stage[:, i % 2, :].rearrange("p (h d) -> p h d", h=HEADS)).then_inc(v_stored[i % 2], 16)
                    v_count = sp.to_reg(b * 8 * V_ITEMS + 8 * V_ITEMS)
                    for i in range(QK_ITEMS):
                        tile, half = i // 2, i % 2
                        pair, dst = tile // 2, (q_dram, k_dram)[tile % 2]
                        sp.wait_ge(qk_lo_done, b * QK_ITEMS + i + 1)
                        for part in range(2):
                            sp.dma_start(dst[part][pair * P:(pair + 1) * P, half * BANK:(half + 1) * BANK],
                                         qk_stage[part][:, i % 2, :].bitcast(F32)).then_inc(qk_stored[i % 2], 16)
                        if i in (1, 2):
                            if i == 1:
                                for slot in range(2):
                                    sp.wait_ge(v_stored[slot], v_count)
                            load_v(i - 1, i - 1)
                        if 5 <= i < 11:
                            if i == 5:
                                for slot in range(2):
                                    sp.wait_ge(qk_stored[slot], b * 16 * QK_ITEMS + 64)
                            load_stack(slice(0, HD), 0, i - 5)
                    for n in range(6):
                        load_stack(slice(HD, P), 1, n)
                    h_count = sp.to_reg(b * KC + KC)
                    qk_count = sp.to_reg(b * 16 * QK_ITEMS + 16 * QK_ITEMS)
                    for slot in range(2):
                        sp.wait_ge(qk_stored[slot], qk_count)
                    sp.wait_ge(h_lo_done, h_count)
                    sp.dma_start(xb[:], x_tiles((b + 1) % B)).then_inc(x_in, 16)
                    with sp.Fori(0, PAIRS - 1) as pair:
                        for e in range(2):
                            head = pair * 2 + 2 + e
                            rows = bass.ds(head * HD, HD)
                            scores_of = sp.to_reg(b * STEPS + pair * 2 * QT + (e + 1) * QT)
                            values_of = sp.to_reg(b * UNITS + pair * 4 + (e + 1) * 2)
                            sp.wait_ge(s_ready, scores_of)
                            for n in range(6):
                                load_stack(rows, e, n)
                            sp.wait_ge(pv_ready, values_of)
                            load_v(head, e)
                    tiles = x_tiles(b)
                    sp.wait_ge(pv_ready, b * UNITS + UNITS - 1)
                    sp.dma_start(res.rearrange("p j n -> p (j n)").rearrange("p (k n) -> p k n", k=KC), tiles).then_inc(xr_in, 16)

            @block.gpsimd
            def _(pool):
                def move_unit(u, slot, head_pair, e, half):
                    if slot is not None:
                        pool.wait_ge(o_done, u + 1)
                    for part in range(2):
                        for c in range(2):
                            dst = ho[part][e * HD:(e + 1) * HD, bass.ds(head_pair, 1),
                                           half * BANK + c * UQ:half * BANK + (c + 1) * UQ]
                            src = o_stage[c * HD:(c + 1) * HD, slot, part:part + 1, :]
                            pool.dma_start(dst.bitcast(F32), src.bitcast(F32)).then_inc(o_moved[slot], 16)

                with pool.Fori(0, B) as b:
                    with pool.Fori(0, PAIRS) as pair:
                        for k in range(4):
                            move_unit(b * UNITS + pair * 4 + k, k % 2, pair, k // 2, k % 2)
                    for j in range(PJ_ITEMS):
                        o, half = j // 2, j % 2
                        pool.wait_ge(pj_done, b * PJ_ITEMS + j + 1)
                        pool.dma_start(x1_dram[b, o * P:(o + 1) * P, half * BANK:(half + 1) * BANK],
                                       res[:, j, :]).then_inc(x1_stored, 16)
                pool.wait_ge(x1_stored, B * PJ_ITEMS * 16)

            @block.scalar
            def _(act):
                def weights_hi(i):
                    act.wait_ge(w_in[i], 16)
                    nc.scalar.activation(w_parts[0][i], w_raw[i], ACT.Copy, scale=HD ** -0.5 if i == 0 else 1.0
                                         ).then_inc(w_hi_done, 1)

                def exp(s, t, u_par):
                    act.wait_ge(max_done, s + 1)
                    nc.scalar.activation(pr[:, t % 2, :],
                                         ps[:, S_BANK + 2 * (t % 2):S_BANK + 2 * (t % 2) + 2, :].rearrange("p a n -> p (a n)"),
                                         ACT.Exp, bias=neg_max[:, t % 4:t % 4 + 1], scale=1.0,
                                         accum_out=row_sum[:, u_par, t % UNIT:t % UNIT + 1]).then_inc(exp_done, 1)

                def bc_copy(u, par):
                    act.wait_ge(pv_ready, u + 1)
                    nc.scalar.activation(r_bc[:, par, :], ps[:, O_BANK + par, UQ:2 * UQ], ACT.Copy).then_inc(bc_done, 1)

                def pair_steps(s0, u0, back, pair, first, last):
                    for i in range(2 * QT):
                        act.wait_ge(t_ready, 2 * s0 + 2 * i + 1)
                        nc.scalar.activation(pt[:, (i // UNIT) % 2, 0:4, (i % UNIT) * P:(i % UNIT + 1) * P],
                                             ps[:, T_BANK, :].rearrange("p (k q) -> p k q", k=4), ACT.Copy).then_inc(t_act, 1)
                        if i % UNIT == UNIT - 1 and not (first and i < UNIT):
                            bc_copy(u0 + i // UNIT - 1, (i // UNIT - 1) % 2)
                        if not (last and i == 2 * QT - 1):
                            exp(s0 + i + 1, (i + 1) % QT, ((i + 1) // UNIT) % 2)

                def split_hi(b, k):
                    act.wait_ge(gn_done, b * KC + k + 1)
                    nc.scalar.activation(ho[0][:, k, :], xb[:, k, :], ACT.Identity, bias=bias_sb[:, k:k + 1],
                                         scale=1.0).then_inc(h_hi_done, 1)

                weights_hi(2)
                for k in range(KC):
                    split_hi(0, k)
                weights_hi(0)
                weights_hi(1)
                weights_hi(3)
                with act.Fori(0, B) as b:
                    for i in range(QK_ITEMS):
                        tile = i // 2
                        col = (tile % 2) * 4 + tile // 2
                        if i == QK_ITEMS - 2:
                            exp(b * STEPS, 0, 0)
                        act.wait_ge(qkv_ready, b * (QK_ITEMS + V_ITEMS) + V_ITEMS + i + 1)
                        if i >= 2:
                            act.wait_ge(qk_stored[i % 2], b * 16 * QK_ITEMS + (i // 2) * 32)
                        nc.scalar.activation(qk_stage[0][:, i % 2, :], ps[:, i % 8, :], ACT.Identity,
                                             bias=bqk_sb[:, col:col + 1], scale=1.0).then_inc(qk_hi_done, 1)
                    over_pairs(act, b, pair_steps)
                    bc_copy(b * UNITS + UNITS - 1, 1)
                    for k in range(KC):
                        if k < KC - 1:
                            act.wait_ge(pj_read, b * (KC - 1) + k + 1)
                        else:
                            act.wait_ge(pj_ready, b * PJ_ITEMS + PJ_ITEMS)
                        split_hi(b + 1, k)

            @block.vector
            def _(dve):
                def weights_lo(i):
                    dve.wait_ge(w_hi_done, (2, 3, 1, 4)[i])
                    if i == 0:
                        last = nc.vector.scalar_tensor_tensor(w_parts[1][i], w_raw[i], HD ** -0.5, w_parts[0][i].bitcast(F32),
                                                              ALU.mult, ALU.subtract)
                    else:
                        last = nc.vector.tensor_tensor(w_parts[1][i], w_raw[i], w_parts[0][i].bitcast(F32), ALU.subtract)
                    last.then_inc(w_lo_done, 1)

                sv = st[:].rearrange("p (s c) -> p s c", s=2)
                means = stt[:, 0:32].rearrange("p (g c) -> p g c", c=GROUP)
                sq3 = sq[:].rearrange("p (g c) -> p g c", c=GROUP)
                group_mean = gs[:, 2:4].unsqueeze(2).broadcast_to([P, 2, GROUP])
                var, root, tmp = gs[:, 4:6], gs[:, 6:8], gs[:, 8:10]

                def norm_stats(b, k, half):
                    if k == 0 and half == 0:
                        dve.wait_ge(x_in, b * 16 + 16)
                    last = nc.vector.bn_stats(bn6[:, k, half, :], xb[:, k, half * BANK:(half + 1) * BANK])
                    if k == KC - 1 and half == 1:
                        last.then_inc(gn_chain, 1)

                def norm_chain(b, part):
                    done = [(0, 6, 10, 12 + 3 * (NEWTON - 2), 12 + 3 * NEWTON)[part]]

                    def wait():
                        done[0] += 1
                        dve.wait_ge(gn_chain, b * GN_LINKS + done[0])

                    if part == 0:
                        wait()
                        nc.vector.memset(sv[:, :, KC:32], 0.0)
                        for k in range(KC):
                            last = nc.vector.bn_aggr(sv[:, :, k], bn6[:, k, :, :].rearrange("p a s -> p (a s)"))
                        last.then_inc(gn_chain, 1)
                        wait()
                        nc.vector.transpose(stt[:], st[:]).then_inc(gn_chain, 1)
                        wait()
                        nc.vector.tensor_reduce(gs[:, 0:2], means, AX_X, ALU.add).then_inc(gn_chain, 1)
                        wait()
                        nc.vector.tensor_scalar(gs[:, 2:4], gs[:, 0:2], 1.0 / GROUP, None, ALU.mult).then_inc(gn_chain, 1)
                        wait()
                        nc.vector.tensor_tensor(sq3, means, group_mean, ALU.subtract).then_inc(gn_chain, 1)
                        wait()
                        nc.vector.tensor_tensor(sq[:], sq[:], sq[:], ALU.mult).then_inc(gn_chain, 1)
                    if part == 1:
                        wait()
                        nc.vector.tensor_tensor(sq[:], sq[:], stt[:, 32:64], ALU.add).then_inc(gn_chain, 1)
                        wait()
                        nc.vector.tensor_reduce(var, sq3, AX_X, ALU.add).then_inc(gn_chain, 1)
                        wait()
                        nc.vector.tensor_scalar(var, var, 1.0 / GROUP, EPS, ALU.mult, ALU.add).then_inc(gn_chain, 1)
                        wait()
                        nc.vector.tensor_scalar(root.bitcast(I32), var.bitcast(I32), 1, None, ALU.logical_shift_right
                                                ).then_inc(gn_chain, 1)
                    if part in (2, 3):
                        if part == 2:
                            wait()
                            nc.vector.tensor_scalar(root.bitcast(I32), root.bitcast(I32), -1.0, float(0x5f3759df),
                                                    ALU.mult, ALU.add).then_inc(gn_chain, 1)
                            wait()
                            nc.vector.tensor_scalar(var, var, -0.5, None, ALU.mult).then_inc(gn_chain, 1)
                        for _ in range(2 if part == 3 else NEWTON - 2):
                            wait()
                            nc.vector.tensor_tensor(tmp, root, root, ALU.mult).then_inc(gn_chain, 1)
                            wait()
                            nc.vector.tensor_tensor(tmp, tmp, var, ALU.mult).then_inc(gn_chain, 1)
                            wait()
                            nc.vector.scalar_tensor_tensor(root, tmp, 1.5, root, ALU.add, ALU.mult).then_inc(gn_chain, 1)
                    if part == 4:
                        wait()
                        nc.vector.tensor_copy(means, group_mean)
                        nc.vector.tensor_copy(stt[:, 32:64].rearrange("p (g c) -> p g c", c=GROUP),
                                              root.unsqueeze(2).broadcast_to([P, 2, GROUP])).then_inc(gn_chain, 1)
                        wait()
                        nc.vector.transpose(gn[:], stt[:]).then_inc(gn_chain, 1)
                        wait()
                        nc.vector.tensor_tensor(gn[:, 32:32 + KC], gn[:, 32:32 + KC], scale_sb, ALU.mult).then_inc(gn_chain, 1)

                def norm_apply(b, k):
                    if k == 0:
                        dve.wait_ge(gn_chain, b * GN_LINKS + GN_LINKS)
                    nc.vector.tensor_scalar(xb[:, k, :], xb[:, k, :], gn[:, k:k + 1], gn[:, 32 + k:33 + k],
                                            ALU.subtract, ALU.mult).then_inc(gn_done, 1)

                def row_max(s, t):
                    dve.wait_ge(s_ready, s + 1)
                    nc.vector.tensor_reduce(neg_max[:, t % 4:t % 4 + 1],
                                            ps[:, S_BANK + 2 * (t % 2):S_BANK + 2 * (t % 2) + 2, :].rearrange("p a n -> p (a n)"),
                                            AX_X, ALU.max, negate=True).then_inc(max_done, 1)

                def inverse_sums(s, u, par):
                    dve.wait_ge(exp_done, s + 1)
                    nc.vector.reciprocal(r_inv[:], row_sum[:, par, :]).then_inc(inv_done, 1)
                    dve.wait_ge(inv_done, u + 1)
                    rv = r_inv[:].rearrange("p (c j) -> p j c", c=2)
                    nc.vector.tensor_copy(r_rep[:].rearrange("p j (c d) -> p j c d", c=2),
                                          rv.unsqueeze(3).broadcast_to([P, 2, 2, HD])).then_inc(rep_done, 1)

                def unit_out(u, par, wait_stage, k_stage):
                    dve.wait_ge(bc_done, u + 1)
                    nc.vector.tensor_tensor(r_bc[:, par, :], ps[:, O_BANK + par, 0:UQ], r_bc[:, par, :], ALU.mult).then_inc(o_chain, 1)
                    if wait_stage:
                        dve.wait_ge(o_moved[par], k_stage)
                    dve.wait_ge(o_chain, 2 * u + 1)
                    nc.vector.tensor_copy(o_stage[:, par, 0, :], r_bc[:, par, :]).then_inc(o_chain, 1)
                    dve.wait_ge(o_chain, 2 * u + 2)
                    nc.vector.tensor_tensor(o_stage[:, par, 1, :], r_bc[:, par, :], o_stage[:, par, 0, :].bitcast(F32),
                                            ALU.subtract).then_inc(o_done, 1)

                def pair_steps(s0, u0, back, pair, first, last):
                    for i in range(2 * QT):
                        if not (last and i == 2 * QT - 1):
                            row_max(s0 + i + 1, (i + 1) % QT)
                        dve.wait_ge(t_ready, 2 * s0 + 2 * i + 2)
                        nc.vector.tensor_copy(pt[:, (i // UNIT) % 2, 4:8, (i % UNIT) * P:(i % UNIT + 1) * P],
                                              ps[:, T_BANK + 1, :].rearrange("p (k q) -> p k q", k=4)).then_inc(t_dve, 1)
                        if i % UNIT == UNIT - 1:
                            k = i // UNIT
                            inverse_sums(s0 + i, u0 + k, k % 2)
                            if not (first and k == 0):
                                former = k - 1 - (k - 1) % 2
                                unit_out(u0 + k - 1, (k - 1) % 2, not (first and k <= 2),
                                         (u0 + former if first else back + 2 + former) * 32)
                        if last:
                            if i % UNIT != UNIT - 1 or i == 2 * QT - 1:
                                piece = i - i // UNIT
                                if piece < 2 * KC:
                                    norm_stats(b_next, piece // 2, piece % 2)
                                else:
                                    norm_chain(b_next, piece - 2 * KC)

                def split_lo(b, k):
                    dve.wait_ge(h_hi_done, b * KC + k + 1)
                    nc.vector.scalar_tensor_tensor(ho[1][:, k, :], xb[:, k, :], bias_sb[:, k:k + 1], ho[0][:, k, :].bitcast(F32),
                                                   ALU.add, ALU.subtract).then_inc(h_lo_done, 1)

                def project_out(b, j):
                    dve.wait_ge(pj_ready, b * PJ_ITEMS + j + 1)
                    nc.vector.scalar_tensor_tensor(res[:, j, :], ps[:, j, :], bproj_sb[:, j // 2:j // 2 + 1], res[:, j, :],
                                                   ALU.add, ALU.add).then_inc(pj_done, 1)

                dve.wait_ge(consts_in, 96)
                nc.vector.tensor_scalar(par[:, 0:4], par[:, 0:4], HD ** -0.5, None, ALU.mult).then_inc(setup_done, 1)
                for k in range(KC):
                    for half in range(HALVES):
                        norm_stats(0, k, half)
                for part in range(5):
                    norm_chain(0, part)
                for k in range(KC):
                    norm_apply(0, k)
                dve.wait_ge(setup_done, 1)
                weights_lo(2)
                for k in range(KC):
                    split_lo(0, k)
                weights_lo(0)
                weights_lo(1)
                weights_lo(3)
                with dve.Fori(0, B) as b:
                    b_next = b + 1
                    for i in range(V_ITEMS):
                        dve.wait_ge(qkv_ready, b * (QK_ITEMS + V_ITEMS) + i + 1)
                        if i >= 2:
                            dve.wait_ge(v_stored[i % 2], b * V_ITEMS * 8 + (i // 2) * 16)
                        nc.vector.tensor_tensor(v_stage[:, i % 2, :], ps[:, i % 4, :], bv_row[:], ALU.add).then_inc(v_done, 1)
                    for i in range(QK_ITEMS):
                        tile = i // 2
                        col = (tile % 2) * 4 + tile // 2
                        if i == QK_ITEMS - 2:
                            row_max(b * STEPS, 0)
                        dve.wait_ge(qk_hi_done, b * QK_ITEMS + i + 1)
                        nc.vector.scalar_tensor_tensor(qk_stage[1][:, i % 2, :], ps[:, i % 8, :], bqk_sb[:, col:col + 1],
                                                       qk_stage[0][:, i % 2, :].bitcast(F32), ALU.add, ALU.subtract
                                                       ).then_inc(qk_lo_done, 1)
                    for slot in range(2):
                        dve.wait_ge(v_stored[slot], b * V_ITEMS * 8 + V_ITEMS * 8)
                    over_pairs(dve, b, pair_steps)
                    unit_out(b * UNITS + UNITS - 1, 1, True, (b * UNITS + UNITS - 2) * 32)
                    for k in range(KC):
                        norm_apply(b + 1, k)
                    for k in range(KC - 1):
                        split_lo(b + 1, k)
                    dve.wait_ge(xr_in, b * 16 + 16)
                    for j in range(4):
                        project_out(b, j)
                    split_lo(b + 1, KC - 1)
                    for j in range(4, PJ_ITEMS):
                        project_out(b, j)
                    dve.wait_ge(x1_stored, b * PJ_ITEMS * 16 + PJ_ITEMS * 16)

            @block.tensor
            def _(pe):
                THREE = ((0, 0), (0, 1), (1, 0))

                def scores(s, e, t):
                    for half in range(HALVES):
                        for n, k_parts in enumerate((k_hh, k_ll)):
                            last = nc.tensor.matmul(ps[:, S_BANK + 2 * (t % 2) + half, :], q_st[:, e, t * P:(t + 1) * P],
                                                    k_parts[:, e, half * BANK:(half + 1) * BANK], start=(n == 0), stop=(n == 1))
                    last.then_inc(s_ready, 1)

                def transposes(t):
                    for j in range(2):
                        for k in range(4):
                            last = nc.tensor.transpose(ps[:, T_BANK + j, k * P:(k + 1) * P],
                                                       pr[:, t % 2, (4 * j + k) * P:(4 * j + k + 1) * P], ident[:])
                        last.then_inc(t_ready, 1)

                def sums_across(par):
                    for j in range(2):
                        last = nc.tensor.transpose(ps[:, O_BANK + par, UQ + j * P:UQ + (j + 1) * P], r_rep[:, j, :], ident[:])
                    last.then_inc(pv_ready, 1)

                def values(par, e, k_tiles):
                    for k in k_tiles:
                        for c in range(2):
                            nc.tensor.matmul(ps[c * HD:(c + 1) * HD, O_BANK + par, 0:UQ], v_sb[:, e, k, :],
                                                    pt[:, par, k, c * UQ:(c + 1) * UQ], start=(k == 0), stop=(k == KT - 1))
                def pair_steps(s0, u0, back, pair, first, last):
                    for i in range(2 * QT):
                        if not (last and i == 2 * QT - 1):
                            j = i + 1
                            if not (first and j == 1):
                                pe.wait_ge(exp_done, s0 + i)
                            if j % QT == 0:
                                e = (j // QT) % 2
                                h = pair * 2 + j // QT
                                pe.wait_ge(qk_loaded[e], head_loads(s0, j // QT) * 96)
                            scores(s0 + j, (j // QT) % 2, j % QT)
                        if not (first and i < UNIT):
                            k = i // UNIT - 1
                            if i % UNIT == 0:
                                pe.wait_ge(t_act, s0 + i)
                                pe.wait_ge(t_dve, s0 + i)
                                pe.wait_ge(v_loaded[(k // 2) % 2], head_loads(s0, k // 2) * 16)
                                if not (first and k < 2):
                                    pe.wait_ge(o_done, u0 + k - 1 if first else back + k + 1)
                            values(k % 2, (k // 2) % 2, range(2 * (i % UNIT), 2 * (i % UNIT) + 2))
                            if i % UNIT == UNIT - 1:
                                pe.wait_ge(rep_done, u0 + k + 1)
                                sums_across(k % 2)
                        pe.wait_ge(exp_done, s0 + i + 1)
                        if not (first and i == 0):
                            pe.wait_ge(t_act, s0 + i)
                            pe.wait_ge(t_dve, s0 + i)
                        if first and i == 0:
                            pe.wait_ge(qk_lo_done, b * QK_ITEMS + 14)
                        transposes(i % QT)
                        if first and i == 0:
                            pe.wait_ge(qk_lo_done, b * QK_ITEMS + 16)

                def head_loads(s0, d):
                    return (s0 + 2 * QT * (d // 2)) // (2 * QT) + 1

                pe.wait_ge(w_lo_done, 1)
                with pe.Fori(0, B) as b:
                    for i in range(V_ITEMS):
                        if i >= 4:
                            pe.wait_ge(v_done, b * V_ITEMS + i - 3)
                        for k in range(KC):
                            if i == 0:
                                pe.wait_ge(h_lo_done, b * KC + k + 1)
                            for n, (h, w) in enumerate(THREE):
                                last = nc.tensor.matmul(ps[:, i % 4, :], ho[h][:, k, i * P:(i + 1) * P],
                                                        wq[w][:, k, 2 * C:3 * C],
                                                        start=(k == 0 and n == 0), stop=(k == KC - 1 and n == 2))
                        last.then_inc(qkv_ready, 1)
                    pe.wait_ge(w_lo_done, 3)
                    for i in range(QK_ITEMS):
                        tile, half = i // 2, i % 2
                        col = ((tile % 2) * 4 + tile // 2) * P
                        if i < 4:
                            pe.wait_ge(v_done, b * V_ITEMS + 5 + i)
                        if i >= 8:
                            pe.wait_ge(qk_lo_done, b * QK_ITEMS + i - 7)
                        if i == QK_ITEMS - 2:
                            pe.wait_ge(qk_lo_done, b * QK_ITEMS + 10)
                            pe.wait_ge(qk_loaded[0], (b * PAIRS + 1) * 96)
                            scores(b * STEPS, 0, 0)
                        for k in range(KC):
                            for n, (w, h) in enumerate(THREE):
                                last = nc.tensor.matmul(ps[:, i % 8, :], wq[w][:, k, col:col + P],
                                                        ho[h][:, k, half * BANK:(half + 1) * BANK],
                                                        start=(k == 0 and n == 0), stop=(k == KC - 1 and n == 2))
                        last.then_inc(qkv_ready, 1)
                    pe.wait_ge(w_lo_done, 4)
                    pe.wait_ge(qk_lo_done, b * QK_ITEMS + 12)
                    over_pairs(pe, b, pair_steps)
                    pe.wait_ge(t_act, b * STEPS + STEPS)
                    pe.wait_ge(t_dve, b * STEPS + STEPS)
                    pe.wait_ge(o_done, b * UNITS + UNITS - 2)
                    values(1, 1, range(KT))
                    pe.wait_ge(rep_done, b * UNITS + UNITS)
                    sums_across(1)
                    for k in range(KC):
                        for slot in range(2):
                            pe.wait_ge(o_moved[slot], (b * UNITS + 4 * (k + 1)) * 32)
                        for j in range(PJ_ITEMS):
                            o, half = j // 2, j % 2
                            if k == 0 and j == 6:
                                pe.wait_ge(o_done, b * UNITS + UNITS)
                            for n, (w, h) in enumerate(THREE):
                                last = nc.tensor.matmul(ps[:, j, :], wp[w][:, k, o * P:(o + 1) * P],
                                                        ho[h][:, k, half * BANK:(half + 1) * BANK],
                                                        start=(k == 0 and n == 0), stop=(k == KC - 1 and n == 2))
                            if k == KC - 1:
                                last.then_inc(pj_ready, 1)
                        if k < KC - 1:
                            last.then_inc(pj_read, 1)
                    pe.wait_ge(pj_done, b * PJ_ITEMS + 1)


def layer1(nc, x1_dram, w_qk, w_v, b_qk, b_v, gamma, eye, out):
    L1_STEPS, L1_UNITS = QT, QT // UNIT

    with ExitStack() as ctx:
        def sb(name, shape, dt=F32):
            return ctx.enter_context(nc.sbuf_tensor(name, shape, dt))

        def sem(name):
            return ctx.enter_context(nc.semaphore(name))

        ps = ctx.enter_context(nc.psum_tensor("ps1", [P, 8, BANK], F32))
        wqk = [sb(f"wqk_{p}", [P, KC, P], F32R) for p in ("hi", "lo")]
        wv = [sb(f"wv_{p}", [P, KC, C], F32R) for p in ("hi", "lo")]
        x_sb = sb("x_sb", [P, KC, N])
        xs = [sb(f"xs_{p}", [P, KC, N], F32R) for p in ("hi", "lo")]
        qk = [sb(f"qk_{p}", [P, N], F32R) for p in ("hi", "lo")]
        q_st = sb("l1_q_st", [P, N], F32R)
        k_hh = sb("l1_k_hh", [P, N], F32R)
        k_ll = sb("l1_k_ll", [P, N], F32R)
        vt = [sb(f"vt_{p}", [P, KT, C], F32R) for p in ("hi", "lo")]
        v_tmp = sb("v_tmp", [P, 3, BANK])
        pt = [sb(f"l1_pt_{p}", [P, KT, UNIT * P], F32R) for p in ("hi", "lo")]
        pr = sb("l1_pr", [P, 2, N])
        x_res = sb("x_res", [P, 2, BANK])
        o_sb = sb("o_sb", [P, 2, BANK])
        r_rep = sb("l1_r_rep", [P, UNIT, P])
        r_bc = sb("l1_r_bc", [P, BANK])
        ident = sb("l1_ident", [P, P])
        bv_row = sb("l1_bv_row", [P, C])
        par = sb("l1_par", [P, 2])
        neg_max = sb("l1_neg_max", [P, 4])
        row_sum = sb("l1_row_sum", [P, 2, UNIT])
        r_inv = sb("l1_r_inv", [P, UNIT])
        bqk_sb, gamma_sb = par[:, 0:1], par[:, 1:2]

        consts_in = sem("l1_consts_in")
        w_in = sem("l1_w_in")
        x_in = sem("l1_x_in")
        w_hi_done = sem("l1_w_hi_done")
        setup_done = sem("l1_setup_done")
        x_hi_done = sem("x_hi_done")
        x_lo_done = sem("x_lo_done")
        proj_ready = sem("proj_ready")
        qk_hi_done = sem("l1_qk_hi_done")
        qk_lo_done = sem("l1_qk_lo_done")
        stacked = sem("stacked")
        v_tmp_done = sem("v_tmp_done")
        v_hi_done = sem("v_hi_done")
        v_lo_done = sem("v_lo_done")
        s_ready = sem("l1_s_ready")
        max_done = sem("l1_max_done")
        exp_done = sem("l1_exp_done")
        t_ready = sem("l1_t_ready")
        t_hi = sem("t_hi")
        t_lo = sem("t_lo")
        inv_done = sem("l1_inv_done")
        rep_done = sem("l1_rep_done")
        bc_ready = sem("bc_ready")
        bc_done = sem("l1_bc_done")
        pv_ready = sem("l1_pv_ready")
        o_chain = sem("l1_o_chain")
        o_done = sem("l1_o_done")
        res_in = [sem(f"res_in_{i}") for i in range(2)]
        out_stored = [sem(f"out_stored_{i}") for i in range(2)]

        OUTS = L1_UNITS * KC

        def x_tiles(b):
            return x1_dram[b].rearrange("(k p) n -> p k n", p=P)

        with nc.Block() as block:

            @block.sync
            def _(sp):
                sp.dma_start(pt_raw_qk(pr), w_qk.rearrange("(k p) o -> p k o", p=P)).then_inc(w_in, 16)
                sp.dma_start(x_sb[:, :, 0:C], w_v.rearrange("(k p) o -> p k o", p=P)).then_inc(w_in, 16)
                sp.dma_start(ident[:], eye).then_inc(consts_in, 16)
                sp.dma_start(bqk_sb, b_qk).then_inc(consts_in, 16)
                sp.dma_start(gamma_sb, gamma.broadcast_to([P, 1])).then_inc(consts_in, 16)
                sp.dma_start(bv_row[:], b_v.broadcast_to([P, C])).then_inc(consts_in, 16)
                sp.wait_ge(setup_done, 2)
                sp.dma_start(x_sb[:], x_tiles(0)).then_inc(x_in, 16)
                with sp.Fori(0, B) as b:
                    sp.wait_ge(x_lo_done, b * KC + KC)
                    sp.dma_start(x_sb[:], x_tiles((b + 1) % B)).then_inc(x_in, 16)
                    sp.wait_ge(qk_lo_done, b * 2 + 2)
                    for dst, src in ((q_st[0:DQK, :], qk[0][0:DQK, :]), (q_st[DQK:P, :], qk[1][0:DQK, :]),
                                     (k_hh[0:DQK, :], qk[0][DQK:P, :]), (k_hh[DQK:P, :], qk[0][DQK:P, :]),
                                     (k_ll[0:DQK, :], qk[1][DQK:P, :]), (k_ll[DQK:P, :], qk[1][DQK:P, :])):
                        sp.dma_start(dst.bitcast(F32), src.bitcast(F32)).then_inc(stacked, 16)
                    for j in range(OUTS):
                        half, c = j // KC, j % KC
                        if j >= 2:
                            sp.wait_ge(o_done, b * OUTS + j - 1)
                        sp.dma_start(x_res[:, j % 2, :], x1_dram[b, c * P:(c + 1) * P, half * BANK:(half + 1) * BANK]
                                     ).then_inc(res_in[j % 2], 16)

            @block.gpsimd
            def _(pool):
                with pool.Fori(0, B) as b:
                    for j in range(OUTS):
                        half, c = j // KC, j % KC
                        pool.wait_ge(o_done, b * OUTS + j + 1)
                        pool.dma_start(out[b, c * P:(c + 1) * P, half * BANK:(half + 1) * BANK],
                                       o_sb[:, j % 2, :]).then_inc(out_stored[j % 2], 16)
                for slot in range(2):
                    pool.wait_ge(out_stored[slot], B * OUTS * 8)

            @block.scalar
            def _(act):
                act.wait_ge(w_in, 32)
                act.wait_ge(consts_in, 64)
                nc.scalar.activation(wqk[0][:], pt_raw_qk(pr), ACT.Copy).then_inc(w_hi_done, 1)
                nc.scalar.activation(wv[0][:], x_sb[:, :, 0:C], ACT.Copy).then_inc(w_hi_done, 1)

                def split_hi(b):
                    act.wait_ge(x_in, b * 16 + 16)
                    for k in range(KC):
                        nc.scalar.activation(xs[0][:, k, :], x_sb[:, k, :], ACT.Copy).then_inc(x_hi_done, 1)

                def exp(s, t):
                    act.wait_ge(max_done, s + 1)
                    nc.scalar.activation(pr[:, t % 2, :],
                                         ps[:, S_BANK + 2 * (t % 2):S_BANK + 2 * (t % 2) + 2, :].rearrange("p a n -> p (a n)"),
                                         ACT.Exp, bias=neg_max[:, t % 4:t % 4 + 1], scale=1.0,
                                         accum_out=row_sum[:, t // UNIT, t % UNIT:t % UNIT + 1]).then_inc(exp_done, 1)

                split_hi(0)
                with act.Fori(0, B) as b:
                    for half in range(HALVES):
                        act.wait_ge(proj_ready, b * (HALVES + V_ITEMS) + half + 1)
                        nc.scalar.activation(qk[0][:, half * BANK:(half + 1) * BANK], ps[:, half, :], ACT.Identity,
                                             bias=bqk_sb, scale=1.0).then_inc(qk_hi_done, 1)
                    for i in range(V_ITEMS):
                        act.wait_ge(v_tmp_done, b * V_ITEMS + i + 1)
                        nc.scalar.activation(vt[0][:, i, :], v_tmp[:, i % 3, :], ACT.Copy).then_inc(v_hi_done, 1)
                    exp(b * L1_STEPS, 0)
                    for i in range(L1_STEPS):
                        for j in range(2):
                            act.wait_ge(t_ready, b * 2 * L1_STEPS + 2 * i + j + 1)
                            nc.scalar.activation(pt[0][:, 4 * j:4 * j + 4, (i % UNIT) * P:(i % UNIT + 1) * P],
                                                 ps[:, T_BANK + j, :].rearrange("p (k q) -> p k q", k=4), ACT.Copy).then_inc(t_hi, 1)
                        if i % UNIT == UNIT - 1:
                            act.wait_ge(bc_ready, b * L1_UNITS + i // UNIT + 1)
                            nc.scalar.activation(r_bc[:], ps[:, O_BANK + i // UNIT, :], ACT.Copy).then_inc(bc_done, 1)
                        if i < L1_STEPS - 1:
                            exp(b * L1_STEPS + i + 1, i + 1)
                    split_hi(b + 1)

            @block.vector
            def _(dve):
                dve.wait_ge(consts_in, 64)
                dve.wait_ge(w_hi_done, 1)
                nc.vector.tensor_tensor(wqk[1][:], pt_raw_qk(pr), wqk[0][:].bitcast(F32), ALU.subtract).then_inc(setup_done, 1)
                dve.wait_ge(w_hi_done, 2)
                nc.vector.tensor_tensor(wv[1][:], x_sb[:, :, 0:C], wv[0][:].bitcast(F32), ALU.subtract).then_inc(setup_done, 1)

                def split_lo(b):
                    for k in range(KC):
                        dve.wait_ge(x_hi_done, b * KC + k + 1)
                        nc.vector.tensor_tensor(xs[1][:, k, :], x_sb[:, k, :], xs[0][:, k, :].bitcast(F32),
                                                ALU.subtract).then_inc(x_lo_done, 1)

                def row_max(s, t):
                    dve.wait_ge(s_ready, s + 1)
                    nc.vector.tensor_reduce(neg_max[:, t % 4:t % 4 + 1],
                                            ps[:, S_BANK + 2 * (t % 2):S_BANK + 2 * (t % 2) + 2, :].rearrange("p a n -> p (a n)"),
                                            AX_X, ALU.max, negate=True).then_inc(max_done, 1)

                split_lo(0)
                with dve.Fori(0, B) as b:
                    for half in range(HALVES):
                        dve.wait_ge(qk_hi_done, b * HALVES + half + 1)
                        nc.vector.scalar_tensor_tensor(qk[1][:, half * BANK:(half + 1) * BANK], ps[:, half, :], bqk_sb,
                                                       qk[0][:, half * BANK:(half + 1) * BANK].bitcast(F32),
                                                       ALU.add, ALU.subtract).then_inc(qk_lo_done, 1)
                    for i in range(V_ITEMS + 1):
                        if i < V_ITEMS:
                            dve.wait_ge(proj_ready, b * (HALVES + V_ITEMS) + HALVES + i + 1)
                            if i >= 3:
                                dve.wait_ge(v_lo_done, b * V_ITEMS + i - 2)
                            nc.vector.tensor_tensor(v_tmp[:, i % 3, :], ps[:, (HALVES + i) % 4, :], bv_row[:],
                                                    ALU.add).then_inc(v_tmp_done, 1)
                        if i > 0:
                            dve.wait_ge(v_hi_done, b * V_ITEMS + i)
                            nc.vector.tensor_tensor(vt[1][:, i - 1, :], v_tmp[:, (i - 1) % 3, :], vt[0][:, i - 1, :].bitcast(F32),
                                                    ALU.subtract).then_inc(v_lo_done, 1)
                    row_max(b * L1_STEPS, 0)
                    for i in range(L1_STEPS):
                        unit = i // UNIT
                        if i % UNIT != UNIT - 1:
                            row_max(b * L1_STEPS + i + 1, i + 1)
                        for j in range(2):
                            dve.wait_ge(t_hi, b * 2 * L1_STEPS + 2 * i + j + 1)
                            nc.vector.tensor_tensor(pt[1][:, 4 * j:4 * j + 4, (i % UNIT) * P:(i % UNIT + 1) * P],
                                                    ps[:, T_BANK + j, :].rearrange("p (k q) -> p k q", k=4),
                                                    pt[0][:, 4 * j:4 * j + 4, (i % UNIT) * P:(i % UNIT + 1) * P].bitcast(F32),
                                                    ALU.subtract).then_inc(t_lo, 1)
                        if i % UNIT == UNIT - 1:
                            dve.wait_ge(exp_done, b * L1_STEPS + i + 1)
                            nc.vector.reciprocal(r_inv[:], row_sum[:, unit, :]).then_inc(inv_done, 1)
                            dve.wait_ge(inv_done, b * L1_UNITS + unit + 1)
                            nc.vector.tensor_copy(r_rep[:], r_inv[:].unsqueeze(2).broadcast_to([P, UNIT, P])).then_inc(rep_done, 1)
                            if i < L1_STEPS - 1:
                                row_max(b * L1_STEPS + i + 1, i + 1)
                            else:
                                split_lo(b + 1)
                            dve.wait_ge(bc_done, b * L1_UNITS + unit + 1)
                            for c in range(KC):
                                j = unit * KC + c
                                dve.wait_ge(pv_ready, b * OUTS + j + 1)
                                if j >= 2:
                                    dve.wait_ge(out_stored[j % 2], b * OUTS * 8 + (j // 2) * 16)
                                nc.vector.tensor_tensor(o_sb[:, j % 2, :], ps[:, O_BANK + (unit + 1 + c) % 2, :], r_bc[:],
                                                        ALU.mult).then_inc(o_chain, 1)
                                dve.wait_ge(o_chain, b * OUTS + j + 1)
                                dve.wait_ge(res_in[j % 2], b * OUTS * 8 + (j // 2) * 16 + 16)
                                nc.vector.scalar_tensor_tensor(o_sb[:, j % 2, :], o_sb[:, j % 2, :], gamma_sb, x_res[:, j % 2, :],
                                                               ALU.mult, ALU.add).then_inc(o_done, 1)
                    for slot in range(2):
                        dve.wait_ge(out_stored[slot], b * OUTS * 8 + OUTS * 8)

            @block.tensor
            def _(pe):
                THREE = ((0, 0), (0, 1), (1, 0))

                def scores(t):
                    for half in range(HALVES):
                        for n, k_parts in enumerate((k_hh, k_ll)):
                            last = nc.tensor.matmul(ps[:, S_BANK + 2 * (t % 2) + half, :], q_st[:, t * P:(t + 1) * P],
                                                    k_parts[:, half * BANK:(half + 1) * BANK], start=(n == 0), stop=(n == 1))
                    last.then_inc(s_ready, 1)

                pe.wait_ge(setup_done, 2)
                with pe.Fori(0, B) as b:
                    pe.wait_ge(x_lo_done, b * KC + KC)
                    for half in range(HALVES):
                        for k in range(KC):
                            for n, (w, h) in enumerate(THREE):
                                last = nc.tensor.matmul(ps[:, half, :], wqk[w][:, k, :], xs[h][:, k, half * BANK:(half + 1) * BANK],
                                                        start=(k == 0 and n == 0), stop=(k == KC - 1 and n == 2))
                        last.then_inc(proj_ready, 1)
                    for i in range(V_ITEMS):
                        if 2 <= i < 4:
                            pe.wait_ge(qk_lo_done, b * HALVES + i - 1)
                        elif i >= 4:
                            pe.wait_ge(v_tmp_done, b * V_ITEMS + i - 3)
                        for k in range(KC):
                            for n, (h, w) in enumerate(THREE):
                                last = nc.tensor.matmul(ps[:, (HALVES + i) % 4, :], xs[h][:, k, i * P:(i + 1) * P], wv[w][:, k, :],
                                                        start=(k == 0 and n == 0), stop=(k == KC - 1 and n == 2))
                        last.then_inc(proj_ready, 1)
                    pe.wait_ge(stacked, b * 96 + 96)
                    pe.wait_ge(v_tmp_done, b * V_ITEMS + V_ITEMS)
                    scores(0)
                    for i in range(L1_STEPS):
                        unit = i // UNIT
                        if i < L1_STEPS - 1:
                            if i > 0:
                                pe.wait_ge(exp_done, b * L1_STEPS + i)
                            scores(i + 1)
                        pe.wait_ge(exp_done, b * L1_STEPS + i + 1)
                        for j in range(2):
                            if i > 0:
                                pe.wait_ge(t_lo, b * 2 * L1_STEPS + 2 * (i - 1) + j + 1)
                            for k in range(4):
                                last = nc.tensor.transpose(ps[:, T_BANK + j, k * P:(k + 1) * P],
                                                           pr[:, i % 2, (4 * j + k) * P:(4 * j + k + 1) * P], ident[:])
                            last.then_inc(t_ready, 1)
                        if i % UNIT == UNIT - 1:
                            pe.wait_ge(rep_done, b * L1_UNITS + unit + 1)
                            if unit == 1:
                                pe.wait_ge(o_done, b * OUTS + KC - 1)
                            for q in range(UNIT):
                                last = nc.tensor.transpose(ps[:, O_BANK + unit, q * P:(q + 1) * P], r_rep[:, q, :], ident[:])
                            last.then_inc(bc_ready, 1)
                            pe.wait_ge(t_lo, b * 2 * L1_STEPS + 2 * i + 2)
                            if unit == 0:
                                pe.wait_ge(v_lo_done, b * V_ITEMS + V_ITEMS)
                            for c in range(KC):
                                j = unit * KC + c
                                if j == 0:
                                    pass
                                elif c == 0:
                                    pe.wait_ge(o_done, b * OUTS + j)
                                elif c == 1:
                                    pe.wait_ge(bc_done, b * L1_UNITS + unit + 1)
                                else:
                                    pe.wait_ge(o_done, b * OUTS + j - 1)
                                for k in range(KT):
                                    for n, (v, p) in enumerate(THREE):
                                        last = nc.tensor.matmul(ps[:, O_BANK + (unit + 1 + c) % 2, :],
                                                                vt[v][:, k, c * P:(c + 1) * P], pt[p][:, k, :],
                                                                start=(k == 0 and n == 0), stop=(k == KT - 1 and n == 2))
                                last.then_inc(pv_ready, 1)


def pt_raw_qk(pr):
    return pr[:].rearrange("p a n -> p (a n)")[:, 0:KC * P].rearrange("p (k o) -> p k o", k=KC)


def build(nc, arrays):
    def dram_in(name):
        return nc.dram_tensor(name, arrays[name].shape, F32, kind="ExternalInput").ap()

    t = {name: dram_in(name) for name in arrays}
    out = nc.dram_tensor("out", (B, C, N), F32, kind="ExternalOutput").ap()
    x1 = nc.dram_tensor("x1_scratch", (B, C, N), F32, kind="Internal").ap()
    layer0(nc, t["x"], t["w_qkv"], t["w_proj"], t["gn_scale"], t["gn_bias"], t["b_qk"], t["b_v"], t["b_proj"], t["eye"], x1)
    layer1(nc, x1, t["w_qk1"], t["w_v1"], t["b_qk1"], t["b_v1"], t["gamma"], t["eye"], out)


def kernel(x, L0_conv_gn_scale, L0_conv_gn_bias, L0_conv_qkv_w, L0_conv_qkv_b, L0_conv_proj_w, L0_conv_proj_b,
           L1_conv_Wq, L1_conv_bq, L1_conv_Wk, L1_conv_bk, L1_conv_Wv, L1_conv_bv, L1_conv_gamma):
    import numpy as np
    import concourse.bacc as bacc
    from concourse.bass_utils import run_bass_kernel_spmd

    def cols(a):
        return np.ascontiguousarray(np.asarray(a).reshape(-1, P).T)

    qkv_b = np.asarray(L0_conv_qkv_b)
    arrays = {
        "x": np.ascontiguousarray(np.asarray(x).reshape(B, C, N)),
        "w_qkv": np.ascontiguousarray(np.asarray(L0_conv_qkv_w).T),
        "w_proj": np.ascontiguousarray(np.asarray(L0_conv_proj_w).T),
        "gn_scale": cols(L0_conv_gn_scale),
        "gn_bias": cols(L0_conv_gn_bias),
        "b_qk": cols(qkv_b[0:2 * C]),
        "b_v": np.ascontiguousarray(qkv_b[2 * C:3 * C].reshape(1, C)),
        "b_proj": cols(L0_conv_proj_b),
        "eye": np.eye(P, dtype=np.float32),
        "w_qk1": np.ascontiguousarray(np.concatenate([np.asarray(L1_conv_Wq), np.asarray(L1_conv_Wk)], axis=0).T),
        "w_v1": np.ascontiguousarray(np.asarray(L1_conv_Wv).T),
        "b_qk1": np.ascontiguousarray(np.concatenate([np.asarray(L1_conv_bq), np.asarray(L1_conv_bk)]).reshape(P, 1)),
        "b_v1": np.ascontiguousarray(np.asarray(L1_conv_bv).reshape(1, C)),
        "gamma": np.ascontiguousarray(np.asarray(L1_conv_gamma).reshape(1, 1)),
    }
    nc = bacc.Bacc("TRN2", target_bir_lowering=False, num_devices=1)
    build(nc, arrays)
    r = run_bass_kernel_spmd(nc, [arrays], core_ids=[0])
    return r.results[0]["out"].reshape(B, C, 32, 32)
```

```python
from contextlib import ExitStack

import concourse.bass as bass
from concourse import mybir

F32 = mybir.dt.float32
F32R = mybir.dt.float32r
I32 = mybir.dt.int32
ALU = mybir.AluOpType
ACT = mybir.ActivationFunctionType
AX_X = mybir.AxisListType.X

P = 128
B, C, N = 8, 512, 1024
KC = C // P
BANK = 512
HALVES = N // BANK
HEADS, HD = 8, 64
PAIRS = HEADS // 2
QT = N // P
KT = N // P
UNIT = 4
UQ = UNIT * P // 2
GROUP = 16
DQK = 64
EPS = 1e-5
S_BANK, T_BANK, O_BANK = 0, 4, 6
QK_ITEMS = 2 * PAIRS * HALVES
V_ITEMS = N // P
PJ_ITEMS = KC * HALVES
STEPS = HEADS * QT
UNITS = STEPS // UNIT


def layer0(nc, x, w_qkv, w_proj, gn_scale, gn_bias, b_qk, b_v, b_proj, eye, x1_dram):
    q_dram = [nc.dram_tensor(f"q_{p}_scratch", (C, N), F32, kind="Internal").ap() for p in ("hi", "lo")]
    k_dram = [nc.dram_tensor(f"k_{p}_scratch", (C, N), F32, kind="Internal").ap() for p in ("hi", "lo")]
    v_dram = nc.dram_tensor("v_scratch", (HEADS, N, HD), F32, kind="Internal").ap()

    with ExitStack() as ctx:
        def sb(name, shape, dt=F32):
            return ctx.enter_context(nc.sbuf_tensor(name, shape, dt))

        def sem(name):
            return ctx.enter_context(nc.semaphore(name))

        ps = ctx.enter_context(nc.psum_tensor("ps0", [P, 8, BANK], F32))
        wq = [sb(f"wqkv_{p}", [P, KC, 3 * C], F32R) for p in ("hi", "lo")]
        wp = [sb(f"wproj_{p}", [P, KC, C], F32R) for p in ("hi", "lo")]
        ho = [sb(f"ho_{p}", [P, KC, N], F32R) for p in ("hi", "lo")]
        q_st = sb("q_st", [P, 2, N], F32R)
        k_hh = sb("k_hh", [P, 2, N], F32R)
        k_ll = sb("k_ll", [P, 2, N], F32R)
        v_sb = sb("v_sb", [P, 2, KT, HD])
        pt = sb("pt", [P, 2, KT, UNIT * P])
        pr = sb("pr", [P, 2, N])
        qk_stage = [sb(f"qk_stage_{p}", [P, 2, BANK], F32R) for p in ("hi", "lo")]
        v_stage = sb("v_stage", [P, 2, BANK])
        xb = sb("xb", [P, KC, N])
        o_stage = sb("o_stage", [P, 2, 2, UQ], F32R)
        r_rep = sb("r_rep", [P, 2, P])
        r_bc = sb("r_bc", [P, 2, UQ])
        ident = sb("ident", [P, P])
        bv_row = sb("bv_row", [P, C])
        par = sb("par", [P, 8 + 3 * KC])
        neg_max = sb("neg_max", [P, 4])
        row_sum = sb("row_sum", [P, 2, UNIT])
        r_inv = sb("r_inv", [P, UNIT])
        bn6 = sb("bn6", [P, KC, 2, 6])
        st = sb("st", [P, 64])
        stt = sb("stt", [P, 64])
        sq = sb("sq", [P, 32])
        gs = sb("gs", [P, 10])
        gn = sb("gn", [P, 64])
        bqk_sb, scale_sb, bias_sb, bproj_sb = par[:, 0:8], par[:, 8:12], par[:, 12:16], par[:, 16:20]

        consts_in = sem("consts_in")
        w_in = [sem(f"w_in_{i}") for i in range(4)]
        x_in = [sem(f"x_in_{k}") for k in range(KC)]
        w_hi_done = sem("w_hi_done")
        w_lo_done = sem("w_lo_done")
        wv_lo_done = sem("wv_lo_done")
        setup_done = sem("setup_done")
        gn_chain = sem("gn_chain")
        gn_done = sem("gn_done")
        h_hi_done = sem("h_hi_done")
        h_lo_done = sem("h_lo_done")
        qkv_ready = sem("qkv_ready")
        qk_hi_done = sem("qk_hi_done")
        qk_lo_done = sem("qk_lo_done")
        v_done = sem("v_done")
        qk_stored = [sem(f"qk_stored_{i}") for i in range(2)]
        v_stored = [sem(f"v_stored_{i}") for i in range(2)]
        qk_loaded = [sem(f"qk_loaded_{i}") for i in range(2)]
        v_loaded = [sem(f"v_loaded_{i}") for i in range(2)]
        s_ready = sem("s_ready")
        max_done = sem("max_done")
        exp_done = sem("exp_done")
        t_ready = sem("t_ready")
        t_act = sem("t_act")
        t_dve = sem("t_dve")
        inv_done = sem("inv_done")
        rep_done = sem("rep_done")
        pv_ready = sem("pv_ready")
        bc_done = sem("bc_done")
        o_chain = sem("o_chain")
        o_done = sem("o_done")
        o_moved = [sem(f"o_moved_{i}") for i in range(2)]
        xr_in = sem("xr_in")
        pj_read = sem("pj_read")
        pj_ready = sem("pj_ready")
        pj_done = sem("pj_done")
        x1_stored = sem("x1_stored")

        raw = pt[:].rearrange("p a k n -> p (a k n)")
        w_raw = [raw[:, i * KC * C:(i + 1) * KC * C].rearrange("p (k o) -> p k o", k=KC) for i in range(4)]
        w_parts = [[wq[part][:, :, i * C:(i + 1) * C] for i in range(3)] + [wp[part][:]] for part in range(2)]
        res = pt[:, 0, :, :].rearrange("p k n -> p (k n)").rearrange("p (j n) -> p j n", n=BANK)

        def x_tiles(b):
            return x[b].rearrange("(k p) n -> p k n", p=P)

        def split_cols(k):
            return [slice(0, BANK), slice(BANK, N)] if k == KC - 1 else [slice(0, N)]

        SPLITS = KC + 1

        def starts(b, pair):
            return b * STEPS + pair * 2 * QT, b * UNITS + pair * 4

        def over_pairs(eng, b, body):
            body(*starts(b, 0), None, 0, True, False)
            with eng.Fori(0, PAIRS - 2) as middle:
                body(*starts(b, middle + 1), b * UNITS + middle * 4 + 2, middle + 1, False, False)
            body(*starts(b, PAIRS - 1), b * UNITS + (PAIRS - 2) * 4 + 2, PAIRS - 1, False, True)

        NEWTON = 3
        GN_LINKS = 16 + 3 * NEWTON

        with nc.Block() as block:

            @block.sync
            def _(sp):
                def load_x(b):
                    for k in range(KC):
                        sp.dma_start(xb[:, k, :], x[b, k * P:(k + 1) * P, :]).then_inc(x_in[k], 16)

                load_x(0)
                sp.dma_start(ident[:], eye).then_inc(consts_in, 16)
                sp.dma_start(bqk_sb, b_qk).then_inc(consts_in, 16)
                sp.dma_start(scale_sb, gn_scale).then_inc(consts_in, 16)
                sp.dma_start(bias_sb, gn_bias).then_inc(consts_in, 16)
                sp.dma_start(bproj_sb, b_proj).then_inc(consts_in, 16)
                sp.dma_start(bv_row[:], b_v.broadcast_to([P, C])).then_inc(consts_in, 16)
                for block_of in (2, 0, 1, 3):
                    src = w_proj if block_of == 3 else w_qkv[:, block_of * C:(block_of + 1) * C]
                    sp.dma_start(w_raw[block_of], src.rearrange("(k p) o -> p k o", p=P)).then_inc(w_in[block_of], 16)

                def load_stack(rows, e, n):
                    lo, hi = slice(0, HD), slice(HD, P)
                    dst, src = ((q_st[lo, e, :], q_dram[0]), (q_st[hi, e, :], q_dram[1]),
                                (k_hh[lo, e, :], k_dram[0]), (k_hh[hi, e, :], k_dram[0]),
                                (k_ll[lo, e, :], k_dram[1]), (k_ll[hi, e, :], k_dram[1]))[n]
                    sp.dma_start(dst.bitcast(F32), src[rows, :]).then_inc(qk_loaded[e], 16)

                def load_v(head, e):
                    sp.dma_start(v_sb[:, e, :, :], v_dram[head].rearrange("(t p) d -> p t d", p=P)).then_inc(v_loaded[e], 16)

                with sp.Fori(0, B) as b:
                    for i in range(V_ITEMS):
                        sp.wait_ge(v_done, b * V_ITEMS + i + 1)
                        sp.dma_start(v_dram[:, i * P:(i + 1) * P, :].rearrange("h p d -> p h d"),
                                     v_stage[:, i % 2, :].rearrange("p (h d) -> p h d", h=HEADS)).then_inc(v_stored[i % 2], 16)
                    v_count = sp.to_reg(b * 8 * V_ITEMS + 8 * V_ITEMS)
                    for i in range(QK_ITEMS):
                        tile, half = i // 2, i % 2
                        pair, dst = tile // 2, (q_dram, k_dram)[tile % 2]
                        sp.wait_ge(qk_lo_done, b * QK_ITEMS + i + 1)
                        for part in range(2):
                            sp.dma_start(dst[part][pair * P:(pair + 1) * P, half * BANK:(half + 1) * BANK],
                                         qk_stage[part][:, i % 2, :].bitcast(F32)).then_inc(qk_stored[i % 2], 16)
                        if i in (1, 2):
                            if i == 1:
                                for slot in range(2):
                                    sp.wait_ge(v_stored[slot], v_count)
                            load_v(i - 1, i - 1)
                        if 5 <= i < 11:
                            if i == 5:
                                for slot in range(2):
                                    sp.wait_ge(qk_stored[slot], b * 16 * QK_ITEMS + 64)
                            load_stack(slice(0, HD), 0, i - 5)
                    for n in range(6):
                        load_stack(slice(HD, P), 1, n)
                    h_count = sp.to_reg(b * SPLITS + SPLITS)
                    qk_count = sp.to_reg(b * 16 * QK_ITEMS + 16 * QK_ITEMS)
                    for slot in range(2):
                        sp.wait_ge(qk_stored[slot], qk_count)
                    sp.wait_ge(h_lo_done, h_count)
                    load_x((b + 1) % B)
                    with sp.Fori(0, PAIRS - 1) as pair:
                        for e in range(2):
                            head = pair * 2 + 2 + e
                            rows = bass.ds(head * HD, HD)
                            scores_of = sp.to_reg(b * STEPS + pair * 2 * QT + (e + 1) * QT)
                            values_of = sp.to_reg(b * UNITS + pair * 4 + (e + 1) * 2)
                            sp.wait_ge(s_ready, scores_of)
                            for n in range(6):
                                load_stack(rows, e, n)
                            sp.wait_ge(pv_ready, values_of)
                            load_v(head, e)
                    sp.wait_ge(pv_ready, b * UNITS + UNITS - 1)
                    sp.dma_start(res.rearrange("p j n -> p (j n)").rearrange("p (k n) -> p k n", k=KC), x_tiles(b)).then_inc(xr_in, 16)
                    for j in range(PJ_ITEMS):
                        o, half = j // 2, j % 2
                        sp.wait_ge(pj_done, b * PJ_ITEMS + j + 1)
                        sp.dma_start(x1_dram[b, o * P:(o + 1) * P, half * BANK:(half + 1) * BANK],
                                     res[:, j, :]).then_inc(x1_stored, 16)
                sp.wait_ge(x1_stored, B * PJ_ITEMS * 16)

            @block.gpsimd
            def _(pool):
                def move_unit(u, slot, head_pair, e, half):
                    pool.wait_ge(o_done, u + 1)
                    for part in range(2):
                        for c in range(2):
                            dst = ho[part][e * HD:(e + 1) * HD, bass.ds(head_pair, 1),
                                           half * BANK + c * UQ:half * BANK + (c + 1) * UQ]
                            src = o_stage[c * HD:(c + 1) * HD, slot, part:part + 1, :]
                            pool.dma_start(dst.bitcast(F32), src.bitcast(F32)).then_inc(o_moved[slot], 16)

                pool.wait_ge(w_hi_done, 1)
                nc.gpsimd.tensor_tensor(w_parts[1][2], w_raw[2], w_parts[0][2].bitcast(F32), ALU.subtract).then_inc(wv_lo_done, 1)
                with pool.Fori(0, B) as b:
                    with pool.Fori(0, PAIRS) as pair:
                        for k in range(4):
                            move_unit(b * UNITS + pair * 4 + k, k % 2, pair, k // 2, k % 2)

            @block.scalar
            def _(act):
                def weights_hi(i):
                    act.wait_ge(w_in[i], 16)
                    nc.scalar.activation(w_parts[0][i], w_raw[i], ACT.Copy, scale=HD ** -0.5 if i == 0 else 1.0
                                         ).then_inc(w_hi_done, 1)

                def exp(s, t, u_par):
                    act.wait_ge(max_done, s + 1)
                    nc.scalar.activation(pr[:, t % 2, :],
                                         ps[:, S_BANK + 2 * (t % 2):S_BANK + 2 * (t % 2) + 2, :].rearrange("p a n -> p (a n)"),
                                         ACT.Exp, bias=neg_max[:, t % 4:t % 4 + 1], scale=1.0,
                                         accum_out=row_sum[:, u_par, t % UNIT:t % UNIT + 1]).then_inc(exp_done, 1)

                def bc_copy(u, par):
                    act.wait_ge(pv_ready, u + 1)
                    nc.scalar.activation(r_bc[:, par, :], ps[:, O_BANK + par, UQ:2 * UQ], ACT.Copy).then_inc(bc_done, 1)

                def pair_steps(s0, u0, back, pair, first, last):
                    for i in range(2 * QT):
                        act.wait_ge(t_ready, 2 * s0 + 2 * i + 1)
                        nc.scalar.activation(pt[:, (i // UNIT) % 2, 0:4, (i % UNIT) * P:(i % UNIT + 1) * P],
                                             ps[:, T_BANK, :].rearrange("p (k q) -> p k q", k=4), ACT.Copy).then_inc(t_act, 1)
                        if i % UNIT == UNIT - 1 and not (first and i < UNIT):
                            bc_copy(u0 + i // UNIT - 1, (i // UNIT - 1) % 2)
                        if not (last and i == 2 * QT - 1):
                            exp(s0 + i + 1, (i + 1) % QT, ((i + 1) // UNIT) % 2)
                        if first and i == 0:
                            qk_hi(b, QK_ITEMS - 1)

                def qk_hi(b, i):
                    tile = i // 2
                    col = (tile % 2) * 4 + tile // 2
                    act.wait_ge(qkv_ready, b * (QK_ITEMS + V_ITEMS) + V_ITEMS + i + 1)
                    if i >= 2:
                        act.wait_ge(qk_stored[i % 2], b * 16 * QK_ITEMS + (i // 2) * 32)
                    nc.scalar.activation(qk_stage[0][:, i % 2, :], ps[:, i % 8, :], ACT.Identity,
                                         bias=bqk_sb[:, col:col + 1], scale=1.0).then_inc(qk_hi_done, 1)

                def split_hi(b, k):
                    act.wait_ge(gn_done, b * KC + k + 1)
                    for cols in split_cols(k):
                        nc.scalar.activation(ho[0][:, k, cols], xb[:, k, cols], ACT.Identity, bias=bias_sb[:, k:k + 1],
                                             scale=1.0).then_inc(h_hi_done, 1)

                weights_hi(2)
                for k in range(KC):
                    split_hi(0, k)
                weights_hi(0)
                weights_hi(1)
                weights_hi(3)
                with act.Fori(0, B) as b:
                    for i in range(QK_ITEMS - 1):
                        if i == QK_ITEMS - 2:
                            exp(b * STEPS, 0, 0)
                        qk_hi(b, i)
                    over_pairs(act, b, pair_steps)
                    bc_copy(b * UNITS + UNITS - 1, 1)
                    for k in range(KC):
                        if k < KC - 1:
                            act.wait_ge(pj_read, b * (KC - 1) + k + 1)
                        else:
                            act.wait_ge(pj_ready, b * PJ_ITEMS + PJ_ITEMS)
                        split_hi(b + 1, k)

            @block.vector
            def _(dve):
                def weights_lo(i):
                    dve.wait_ge(w_hi_done, (2, 3, None, 4)[i])
                    if i == 0:
                        last = nc.vector.scalar_tensor_tensor(w_parts[1][i], w_raw[i], HD ** -0.5, w_parts[0][i].bitcast(F32),
                                                              ALU.mult, ALU.subtract)
                    else:
                        last = nc.vector.tensor_tensor(w_parts[1][i], w_raw[i], w_parts[0][i].bitcast(F32), ALU.subtract)
                    last.then_inc(w_lo_done, 1)

                sv = st[:].rearrange("p (s c) -> p s c", s=2)
                means = stt[:, 0:32].rearrange("p (g c) -> p g c", c=GROUP)
                sq3 = sq[:].rearrange("p (g c) -> p g c", c=GROUP)
                group_mean = gs[:, 2:4].unsqueeze(2).broadcast_to([P, 2, GROUP])
                var, root, tmp = gs[:, 4:6], gs[:, 6:8], gs[:, 8:10]

                def norm_stats(b, k, half):
                    if half == 0:
                        dve.wait_ge(x_in[k], b * 16 + 16)
                    last = nc.vector.bn_stats(bn6[:, k, half, :], xb[:, k, half * BANK:(half + 1) * BANK])
                    if k == KC - 1 and half == 1:
                        last.then_inc(gn_chain, 1)

                def norm_chain(b, part):
                    done = [(0, 3, 6, 10, 12 + 3 * NEWTON)[part]]

                    def wait():
                        done[0] += 1
                        dve.wait_ge(gn_chain, b * GN_LINKS + done[0])

                    if part == 0:
                        wait()
                        nc.vector.memset(sv[:, :, KC:32], 0.0)
                        for k in range(KC):
                            last = nc.vector.bn_aggr(sv[:, :, k], bn6[:, k, :, :].rearrange("p a s -> p (a s)"))
                        last.then_inc(gn_chain, 1)
                        wait()
                        nc.vector.transpose(stt[:], st[:]).then_inc(gn_chain, 1)
                        wait()
                        nc.vector.tensor_reduce(gs[:, 0:2], means, AX_X, ALU.add).then_inc(gn_chain, 1)
                    if part == 1:
                        wait()
                        nc.vector.tensor_scalar(gs[:, 2:4], gs[:, 0:2], 1.0 / GROUP, None, ALU.mult).then_inc(gn_chain, 1)
                        wait()
                        nc.vector.tensor_tensor(sq3, means, group_mean, ALU.subtract).then_inc(gn_chain, 1)
                        wait()
                        nc.vector.tensor_tensor(sq[:], sq[:], sq[:], ALU.mult).then_inc(gn_chain, 1)
                    if part == 2:
                        wait()
                        nc.vector.tensor_tensor(sq[:], sq[:], stt[:, 32:64], ALU.add).then_inc(gn_chain, 1)
                        wait()
                        nc.vector.tensor_reduce(var, sq3, AX_X, ALU.add).then_inc(gn_chain, 1)
                        wait()
                        nc.vector.tensor_scalar(var, var, 1.0 / GROUP, EPS, ALU.mult, ALU.add).then_inc(gn_chain, 1)
                        wait()
                        nc.vector.tensor_scalar(root.bitcast(I32), var.bitcast(I32), 1, None, ALU.logical_shift_right
                                                ).then_inc(gn_chain, 1)
                    if part == 3:
                        wait()
                        nc.vector.tensor_scalar(root.bitcast(I32), root.bitcast(I32), -1.0, float(0x5f3759df),
                                                ALU.mult, ALU.add).then_inc(gn_chain, 1)
                        wait()
                        nc.vector.tensor_scalar(var, var, -0.5, None, ALU.mult).then_inc(gn_chain, 1)
                        for _ in range(NEWTON):
                            wait()
                            nc.vector.tensor_tensor(tmp, root, root, ALU.mult).then_inc(gn_chain, 1)
                            wait()
                            nc.vector.tensor_tensor(tmp, tmp, var, ALU.mult).then_inc(gn_chain, 1)
                            wait()
                            nc.vector.scalar_tensor_tensor(root, tmp, 1.5, root, ALU.add, ALU.mult).then_inc(gn_chain, 1)
                    if part == 4:
                        wait()
                        nc.vector.tensor_copy(means, group_mean)
                        nc.vector.tensor_copy(stt[:, 32:64].rearrange("p (g c) -> p g c", c=GROUP),
                                              root.unsqueeze(2).broadcast_to([P, 2, GROUP])).then_inc(gn_chain, 1)
                        wait()
                        nc.vector.transpose(gn[:], stt[:]).then_inc(gn_chain, 1)
                        wait()
                        nc.vector.tensor_tensor(gn[:, 32:32 + KC], gn[:, 32:32 + KC], scale_sb, ALU.mult).then_inc(gn_chain, 1)

                def norm_apply(b, k):
                    if k == 0:
                        dve.wait_ge(gn_chain, b * GN_LINKS + GN_LINKS)
                    nc.vector.tensor_scalar(xb[:, k, :], xb[:, k, :], gn[:, k:k + 1], gn[:, 32 + k:33 + k],
                                            ALU.subtract, ALU.mult).then_inc(gn_done, 1)

                def row_max(s, t):
                    dve.wait_ge(s_ready, s + 1)
                    nc.vector.tensor_reduce(neg_max[:, t % 4:t % 4 + 1],
                                            ps[:, S_BANK + 2 * (t % 2):S_BANK + 2 * (t % 2) + 2, :].rearrange("p a n -> p (a n)"),
                                            AX_X, ALU.max, negate=True).then_inc(max_done, 1)

                def inverse_sums(exps, units, par):
                    dve.wait_ge(exp_done, exps)
                    nc.vector.reciprocal(r_inv[:], row_sum[:, par, :]).then_inc(inv_done, 1)
                    dve.wait_ge(inv_done, units)
                    rv = r_inv[:].rearrange("p (c j) -> p j c", c=2)
                    nc.vector.tensor_copy(r_rep[:].rearrange("p j (c d) -> p j c d", c=2),
                                          rv.unsqueeze(3).broadcast_to([P, 2, 2, HD])).then_inc(rep_done, 1)

                def unit_out(u, par, wait_stage, k_stage):
                    dve.wait_ge(bc_done, u + 1)
                    nc.vector.tensor_tensor(r_bc[:, par, :], ps[:, O_BANK + par, 0:UQ], r_bc[:, par, :], ALU.mult).then_inc(o_chain, 1)
                    if wait_stage:
                        dve.wait_ge(o_moved[par], k_stage)
                    dve.wait_ge(o_chain, 2 * u + 1)
                    nc.vector.tensor_copy(o_stage[:, par, 0, :], r_bc[:, par, :]).then_inc(o_chain, 1)
                    dve.wait_ge(o_chain, 2 * u + 2)
                    nc.vector.tensor_tensor(o_stage[:, par, 1, :], r_bc[:, par, :], o_stage[:, par, 0, :].bitcast(F32),
                                            ALU.subtract).then_inc(o_done, 1)

                def pair_steps(s0, u0, back, pair, first, last):
                    for i in range(2 * QT):
                        if not (last and i == 2 * QT - 1) and not (first and i == 1):
                            row_max(s0 + i + 1, (i + 1) % QT)
                        m = i // UNIT
                        if i % UNIT == 0:
                            if not (first and m == 0):
                                inverse_sums(s0 + i, u0 + m if first else back + m + 2, (m - 1) % 2)
                            if not first:
                                unit_out(back + m, m % 2, True, (back + m - m % 2) * 32)
                            elif m >= 2:
                                unit_out(u0 + m - 2, m % 2, False, None)
                        dve.wait_ge(t_ready, 2 * s0 + 2 * i + 2)
                        nc.vector.tensor_copy(pt[:, m % 2, 4:8, (i % UNIT) * P:(i % UNIT + 1) * P],
                                              ps[:, T_BANK + 1, :].rearrange("p (k q) -> p k q", k=4)).then_inc(t_dve, 1)
                        if first and i == 0:
                            row_max(s0 + 2, 2)
                            qk_lo(b, QK_ITEMS - 1)
                        if last:
                            if i == 2 * QT - 1:
                                inverse_sums(s0 + i + 1, u0 + 4, 1)
                                unit_out(u0 + 2, 0, True, (u0 + 2) * 32)
                        if first and i in (9, 10, 13, 14):
                            piece = (9, 10, 13, 14).index(i)
                            norm_stats(b_next, piece // 2, piece % 2)
                        if last and i in (2, 3, 6, 7):
                            piece = (2, 3, 6, 7).index(i)
                            norm_stats(b_next, 2 + piece // 2, piece % 2)
                        if last and i in (10, 11, 14):
                            norm_chain(b_next, (10, 11, 14).index(i))

                def qk_lo(b, i):
                    tile = i // 2
                    col = (tile % 2) * 4 + tile // 2
                    dve.wait_ge(qk_hi_done, b * QK_ITEMS + i + 1)
                    nc.vector.scalar_tensor_tensor(qk_stage[1][:, i % 2, :], ps[:, i % 8, :], bqk_sb[:, col:col + 1],
                                                   qk_stage[0][:, i % 2, :].bitcast(F32), ALU.add, ALU.subtract
                                                   ).then_inc(qk_lo_done, 1)

                def split_lo(b, k):
                    for n, cols in enumerate(split_cols(k)):
                        dve.wait_ge(h_hi_done, b * SPLITS + k + n + 1)
                        nc.vector.scalar_tensor_tensor(ho[1][:, k, cols], xb[:, k, cols], bias_sb[:, k:k + 1],
                                                       ho[0][:, k, cols].bitcast(F32), ALU.add, ALU.subtract
                                                       ).then_inc(h_lo_done, 1)

                def project_out(b, j):
                    dve.wait_ge(pj_ready, b * PJ_ITEMS + j + 1)
                    nc.vector.scalar_tensor_tensor(res[:, j, :], ps[:, j, :], bproj_sb[:, j // 2:j // 2 + 1], res[:, j, :],
                                                   ALU.add, ALU.add).then_inc(pj_done, 1)

                for k in range(KC):
                    for half in range(HALVES):
                        norm_stats(0, k, half)
                dve.wait_ge(consts_in, 96)
                nc.vector.tensor_scalar(par[:, 0:4], par[:, 0:4], HD ** -0.5, None, ALU.mult).then_inc(setup_done, 1)
                for part in range(5):
                    norm_chain(0, part)
                for k in range(KC):
                    norm_apply(0, k)
                dve.wait_ge(setup_done, 1)
                for k in range(KC):
                    split_lo(0, k)
                weights_lo(0)
                weights_lo(1)
                weights_lo(3)
                with dve.Fori(0, B) as b:
                    b_next = b + 1
                    for i in range(V_ITEMS):
                        dve.wait_ge(qkv_ready, b * (QK_ITEMS + V_ITEMS) + i + 1)
                        if i >= 2:
                            dve.wait_ge(v_stored[i % 2], b * V_ITEMS * 8 + (i // 2) * 16)
                        nc.vector.tensor_tensor(v_stage[:, i % 2, :], ps[:, i % 4, :], bv_row[:], ALU.add).then_inc(v_done, 1)
                    for i in range(QK_ITEMS - 1):
                        if i == QK_ITEMS - 2:
                            row_max(b * STEPS, 0)
                        qk_lo(b, i)
                    for slot in range(2):
                        dve.wait_ge(v_stored[slot], b * V_ITEMS * 8 + V_ITEMS * 8)
                    over_pairs(dve, b, pair_steps)
                    unit_out(b * UNITS + UNITS - 1, 1, True, (b * UNITS + UNITS - 2) * 32)
                    for part in range(3, 5):
                        norm_chain(b_next, part)
                    for k in range(KC):
                        norm_apply(b + 1, k)
                    for k in range(KC - 1):
                        split_lo(b + 1, k)
                    dve.wait_ge(xr_in, b * 16 + 16)
                    for j in range(4):
                        project_out(b, j)
                    split_lo(b + 1, KC - 1)
                    for j in range(4, PJ_ITEMS):
                        project_out(b, j)
                    dve.wait_ge(x1_stored, b * PJ_ITEMS * 16 + PJ_ITEMS * 16)

            @block.tensor
            def _(pe):
                THREE = ((0, 0), (0, 1), (1, 0))

                def queries_keys(b, i):
                    tile, half = i // 2, i % 2
                    col = ((tile % 2) * 4 + tile // 2) * P
                    if i < 4:
                        pe.wait_ge(v_done, b * V_ITEMS + 5 + i)
                    if i >= 8:
                        pe.wait_ge(qk_lo_done, b * QK_ITEMS + i - 7)
                    for k in range(KC):
                        for n, (w, h) in enumerate(THREE):
                            last = nc.tensor.matmul(ps[:, i % 8, :], wq[w][:, k, col:col + P],
                                                    ho[h][:, k, half * BANK:(half + 1) * BANK],
                                                    start=(k == 0 and n == 0), stop=(k == KC - 1 and n == 2))
                    last.then_inc(qkv_ready, 1)

                def scores(s, e, t):
                    for half in range(HALVES):
                        for n, k_parts in enumerate((k_hh, k_ll)):
                            last = nc.tensor.matmul(ps[:, S_BANK + 2 * (t % 2) + half, :], q_st[:, e, t * P:(t + 1) * P],
                                                    k_parts[:, e, half * BANK:(half + 1) * BANK], start=(n == 0), stop=(n == 1))
                    last.then_inc(s_ready, 1)

                def transposes(t):
                    for j in range(2):
                        for k in range(4):
                            last = nc.tensor.transpose(ps[:, T_BANK + j, k * P:(k + 1) * P],
                                                       pr[:, t % 2, (4 * j + k) * P:(4 * j + k + 1) * P], ident[:])
                        last.then_inc(t_ready, 1)

                def sums_across(par):
                    for j in range(2):
                        last = nc.tensor.transpose(ps[:, O_BANK + par, UQ + j * P:UQ + (j + 1) * P], r_rep[:, j, :], ident[:])
                    last.then_inc(pv_ready, 1)

                def values(par, e, k_tiles):
                    for k in k_tiles:
                        for c in range(2):
                            nc.tensor.matmul(ps[c * HD:(c + 1) * HD, O_BANK + par, 0:UQ], v_sb[:, e, k, :],
                                             pt[:, par, k, c * UQ:(c + 1) * UQ], start=(k == 0), stop=(k == KT - 1))

                def project(k, items):
                    for j in items:
                        o, half = j // 2, j % 2
                        for n, (w, h) in enumerate(THREE):
                            last = nc.tensor.matmul(ps[:, j, :], wp[w][:, k, o * P:(o + 1) * P],
                                                    ho[h][:, k, half * BANK:(half + 1) * BANK],
                                                    start=(k == 0 and n == 0), stop=(k == KC - 1 and n == 2))
                        if k == KC - 1:
                            last.then_inc(pj_ready, 1)
                        elif j == PJ_ITEMS - 1:
                            last.then_inc(pj_read, 1)

                def pair_steps(s0, u0, back, pair, first, last):
                    for i in range(2 * QT):
                        if not (last and i == 2 * QT - 1) and not (first and i == 1):
                            j = i + 1
                            if not (first and j == 1):
                                pe.wait_ge(exp_done, s0 + i)
                            if j % QT == 0:
                                e = (j // QT) % 2
                                pe.wait_ge(qk_loaded[e], head_loads(s0, j // QT) * 96)
                            scores(s0 + j, (j // QT) % 2, j % QT)
                        if not (first and i < UNIT):
                            k = i // UNIT - 1
                            if i % UNIT == 0:
                                pe.wait_ge(t_act, s0 + i)
                                pe.wait_ge(v_loaded[(k // 2) % 2], head_loads(s0, k // 2) * 16)
                                if not (first and k < 2):
                                    pe.wait_ge(o_done, u0 + k - 1 if first else back + k + 1)
                            values(k % 2, (k // 2) % 2, range(2 * (i % UNIT), 2 * (i % UNIT) + 2))
                            if i % UNIT == UNIT - 1:
                                pe.wait_ge(rep_done, u0 + k + 1)
                                sums_across(k % 2)
                        if last and i == 2 * QT - 1:
                            for slot in range(2):
                                pe.wait_ge(o_moved[slot], (b * UNITS + 4) * 32)
                            pe.wait_ge(exp_done, s0 + i)
                            project(0, range(0, 2))
                        pe.wait_ge(exp_done, s0 + i + 1)
                        if not (first and i == 0):
                            pe.wait_ge(t_act, s0 + i)
                            pe.wait_ge(t_dve, s0 + i)
                        if first and i == 0:
                            pe.wait_ge(qk_lo_done, b * QK_ITEMS + 14)
                        transposes(i % QT)
                        if last and i == 2 * QT - 1:
                            project(0, range(2, 4))
                        if first and i == 0:
                            scores(s0 + 2, 0, 2)
                            queries_keys(b, QK_ITEMS - 1)
                        if first and i == UNIT - 1:
                            pe.wait_ge(qk_lo_done, b * QK_ITEMS + 16)

                def head_loads(s0, d):
                    return (s0 + 2 * QT * (d // 2)) // (2 * QT) + 1

                pe.wait_ge(wv_lo_done, 1)
                with pe.Fori(0, B) as b:
                    for i in range(V_ITEMS):
                        if i >= 4:
                            pe.wait_ge(v_done, b * V_ITEMS + i - 3)
                        for k in range(KC):
                            if i == 0:
                                pe.wait_ge(h_lo_done, b * SPLITS + k + 1)
                            if i == V_ITEMS // 2 and k == KC - 1:
                                pe.wait_ge(h_lo_done, b * SPLITS + SPLITS)
                            for n, (h, w) in enumerate(THREE):
                                last = nc.tensor.matmul(ps[:, i % 4, :], ho[h][:, k, i * P:(i + 1) * P],
                                                        wq[w][:, k, 2 * C:3 * C],
                                                        start=(k == 0 and n == 0), stop=(k == KC - 1 and n == 2))
                        last.then_inc(qkv_ready, 1)
                    pe.wait_ge(w_lo_done, 2)
                    for i in range(QK_ITEMS - 1):
                        if i == QK_ITEMS - 2:
                            pe.wait_ge(qk_lo_done, b * QK_ITEMS + 10)
                            pe.wait_ge(qk_loaded[0], (b * PAIRS + 1) * 96)
                            scores(b * STEPS, 0, 0)
                        queries_keys(b, i)
                    pe.wait_ge(w_lo_done, 3)
                    pe.wait_ge(qk_lo_done, b * QK_ITEMS + 12)
                    over_pairs(pe, b, pair_steps)
                    pe.wait_ge(o_done, b * UNITS + UNITS - 2)
                    pe.wait_ge(t_act, b * STEPS + STEPS)
                    values(1, 1, range(KT // 2))
                    pe.wait_ge(t_dve, b * STEPS + STEPS)
                    values(1, 1, range(KT // 2, KT))
                    pe.wait_ge(rep_done, b * UNITS + UNITS)
                    sums_across(1)
                    project(0, range(4, 6))
                    for slot in range(2):
                        pe.wait_ge(o_moved[slot], (b * UNITS + 4 * 2) * 32)
                    project(1, range(0, 6))
                    pe.wait_ge(o_done, b * UNITS + UNITS)
                    project(0, range(6, 8))
                    project(1, range(6, 8))
                    for k in range(2, KC):
                        for slot in range(2):
                            pe.wait_ge(o_moved[slot], (b * UNITS + 4 * (k + 1)) * 32)
                        project(k, range(PJ_ITEMS))
                    pe.wait_ge(pj_done, b * PJ_ITEMS + 1)


def layer1(nc, x1_dram, w_qk, w_v, b_qk, b_v, gamma, eye, out):
    L1_STEPS, L1_UNITS = QT, QT // UNIT
    OUTS = L1_UNITS * KC
    LAST = L1_STEPS - 1
    SPLITS = ((0, 1), (2, 3), (), ())

    with ExitStack() as ctx:
        def sb(name, shape, dt=F32):
            return ctx.enter_context(nc.sbuf_tensor(name, shape, dt))

        def sem(name):
            return ctx.enter_context(nc.semaphore(name))

        ps = ctx.enter_context(nc.psum_tensor("ps1", [P, 8, BANK], F32))
        wqk = [sb(f"wqk_{p}", [P, KC, P], F32R) for p in ("hi", "lo")]
        wv = [sb(f"wv_{p}", [P, KC, C], F32R) for p in ("hi", "lo")]
        x_sb = sb("x_sb", [P, 2, N])
        xs = [sb(f"xs_{p}", [P, KC, N], F32R) for p in ("hi", "lo")]
        q_lo = sb("q_lo", [DQK, N], F32R)
        q_st = sb("l1_q_st", [P, N], F32R)
        k_hh = sb("l1_k_hh", [P, N], F32R)
        k_ll = sb("l1_k_ll", [P, N], F32R)
        vt = [sb(f"vt_{p}", [P, KT, C], F32R) for p in ("hi", "lo")]
        v_tmp = sb("v_tmp", [P, 3, BANK])
        pt = [sb(f"l1_pt_{p}", [P, 2, KT, UNIT * P], F32R) for p in ("hi", "lo")]
        pr = sb("l1_pr", [P, 2, N])
        x_res = sb("x_res", [P, 2, BANK])
        o_sb = sb("o_sb", [P, 2, BANK])
        r_rep = sb("l1_r_rep", [P, UNIT, P])
        r_bc = sb("l1_r_bc", [P, 2, BANK])
        ident = sb("l1_ident", [P, P])
        bv_row = sb("l1_bv_row", [P, C])
        par = sb("l1_par", [P, 2])
        neg_max = sb("l1_neg_max", [P, 4])
        row_sum = sb("l1_row_sum", [P, 2, UNIT])
        r_inv = sb("l1_r_inv", [P, UNIT])
        bqk_sb, gamma_sb = par[:, 0:1], par[:, 1:2]

        raw_qk = v_tmp[:].rearrange("p a n -> p (a n)")[:, 0:KC * P].rearrange("p (k o) -> p k o", k=KC)
        first_x = pt[1][:, 1, :, :].bitcast(F32).rearrange("p t q -> p (t q)").rearrange("p (k n) -> p k n", k=KC)
        raw_v = pr[:].rearrange("p a n -> p (a n)").rearrange("p (k o) -> p k o", k=KC)

        consts_in = sem("l1_consts_in")
        wqk_in = sem("wqk_in")
        wv_in = sem("wv_in")
        first_x_in = [sem(f"first_x_in_{k}") for k in range(KC)]
        x_in = [sem(f"l1_x_in_{i}") for i in range(2)]
        w_hi_done = sem("l1_w_hi_done")
        setup_done = sem("l1_setup_done")
        x_hi_done = sem("x_hi_done")
        x_lo_done = sem("x_lo_done")
        qk_ready = sem("qk_ready")
        v_ready = sem("v_ready")
        qk_hi_done = sem("l1_qk_hi_done")
        qk_lo_done = sem("l1_qk_lo_done")
        stacked = sem("stacked")
        v_tmp_done = sem("v_tmp_done")
        v_hi_done = sem("v_hi_done")
        v_lo_done = sem("v_lo_done")
        s_ready = sem("l1_s_ready")
        max_done = sem("l1_max_done")
        exp_done = sem("l1_exp_done")
        t_ready = sem("l1_t_ready")
        t_hi = sem("t_hi")
        t_lo = sem("t_lo")
        inv_done = sem("l1_inv_done")
        rep_done = sem("l1_rep_done")
        bc_ready = sem("bc_ready")
        bc_done = sem("l1_bc_done")
        pv_ready = sem("l1_pv_ready")
        o_scaled = sem("o_scaled")
        o_done = sem("l1_o_done")
        res_in = [sem(f"res_in_{i}") for i in range(2)]
        out_stored = [sem(f"out_stored_{i}") for i in range(2)]

        with nc.Block() as block:

            @block.sync
            def _(sp):
                def load_x(b, k):
                    sp.dma_start(x_sb[:, k % 2, :], x1_dram[b, k * P:(k + 1) * P, :]).then_inc(x_in[k % 2], 16)

                def load_res(b, j):
                    half, c = j // KC, j % KC
                    sp.dma_start(x_res[:, j % 2, :], x1_dram[b, c * P:(c + 1) * P, half * BANK:(half + 1) * BANK]
                                 ).then_inc(res_in[j % 2], 16)

                sp.dma_start(raw_qk, w_qk.rearrange("(k p) o -> p k o", p=P)).then_inc(wqk_in, 16)
                for k in range(KC):
                    sp.dma_start(first_x[:, k, :], x1_dram[0, k * P:(k + 1) * P, :]).then_inc(first_x_in[k], 16)
                sp.dma_start(bqk_sb, b_qk).then_inc(consts_in, 16)
                sp.dma_start(gamma_sb, gamma.broadcast_to([P, 1])).then_inc(consts_in, 16)
                sp.dma_start(bv_row[:], b_v.broadcast_to([P, C])).then_inc(consts_in, 16)
                sp.dma_start(ident[:], eye).then_inc(consts_in, 16)
                sp.dma_start(raw_v, w_v.rearrange("(k p) o -> p k o", p=P)).then_inc(wv_in, 16)
                for j in range(2):
                    load_res(0, j)
                with sp.Fori(0, B) as b:
                    b_next = (b + 1) % B
                    for k in range(2):
                        sp.wait_ge(x_lo_done, b * KC + k + 3)
                        load_x(b_next, k)
                    for half in range(HALVES):
                        cols = slice(half * BANK, (half + 1) * BANK)
                        sp.wait_ge(qk_lo_done, b * 2 + half + 1)
                        for dst, src in ((q_st[DQK:P, cols], q_lo[:, cols]), (k_hh[0:DQK, cols], k_hh[DQK:P, cols]),
                                         (k_ll[0:DQK, cols], k_ll[DQK:P, cols])):
                            sp.dma_start(dst.bitcast(F32), src.bitcast(F32)).then_inc(stacked, 16)
                    for j in range(OUTS):
                        half, c = j // KC, j % KC
                        if j == 0:
                            for k in range(2, KC):
                                sp.wait_ge(x_lo_done, b * KC + KC + k - 1)
                                load_x(b_next, k)
                        if j >= OUTS - 2:
                            stored = sp.to_reg(b * OUTS * 8 + OUTS * 8)
                        sp.wait_ge(o_done, b * OUTS + j + 1)
                        sp.dma_start(out[b, c * P:(c + 1) * P, half * BANK:(half + 1) * BANK],
                                     o_sb[:, j % 2, :]).then_inc(out_stored[j % 2], 16)
                        if j < OUTS - 2:
                            load_res(b, j + 2)
                        else:
                            sp.wait_ge(out_stored[j % 2], stored)
                            load_res(b_next, j % 2)
                for slot in range(2):
                    sp.wait_ge(res_in[slot], B * OUTS * 8 + 16)

            @block.scalar
            def _(act):
                def split_hi(b_next, k):
                    act.wait_ge(x_in[k % 2], (b_next - 1) * 32 + (k // 2) * 16 + 16)
                    nc.scalar.activation(xs[0][:, k, :], x_sb[:, k % 2, :], ACT.Copy).then_inc(x_hi_done, 1)

                def v_hi(b, i):
                    act.wait_ge(v_tmp_done, b * V_ITEMS + i + 1)
                    nc.scalar.activation(vt[0][:, i, :], v_tmp[:, i % 3, :], ACT.Copy).then_inc(v_hi_done, 1)

                def exp(b, t):
                    act.wait_ge(max_done, b * L1_STEPS + t + 1)
                    nc.scalar.activation(pr[:, t % 2, :],
                                         ps[:, S_BANK + 2 * (t % 2):S_BANK + 2 * (t % 2) + 2, :].rearrange("p a n -> p (a n)"),
                                         ACT.Exp, bias=neg_max[:, t % 4:t % 4 + 1], scale=1.0,
                                         accum_out=row_sum[:, t // UNIT, t % UNIT:t % UNIT + 1]).then_inc(exp_done, 1)

                def probs_hi(b, t):
                    for j in range(2):
                        act.wait_ge(t_ready, b * 2 * L1_STEPS + 2 * t + j + 1)
                        nc.scalar.activation(pt[0][:, t // UNIT, 4 * j:4 * j + 4, (t % UNIT) * P:(t % UNIT + 1) * P],
                                             ps[:, T_BANK + j, :].rearrange("p (k q) -> p k q", k=4), ACT.Copy).then_inc(t_hi, 1)

                def bc_copy(b, unit):
                    act.wait_ge(bc_ready, b * L1_UNITS + unit + 1)
                    nc.scalar.activation(r_bc[:, unit, :], ps[:, T_BANK, :], ACT.Copy).then_inc(bc_done, 1)

                act.wait_ge(wqk_in, 16)
                nc.scalar.activation(wqk[0][:], raw_qk, ACT.Copy).then_inc(w_hi_done, 1)
                for k in range(KC):
                    act.wait_ge(first_x_in[k], 16)
                    nc.scalar.activation(xs[0][:, k, :], first_x[:, k, :], ACT.Copy).then_inc(x_hi_done, 1)
                act.wait_ge(wv_in, 16)
                for k in range(KC):
                    nc.scalar.activation(wv[0][:, k, :], raw_v[:, k, :], ACT.Copy).then_inc(w_hi_done, 1)
                act.wait_ge(consts_in, 64)
                with act.Fori(0, B) as b:
                    for half in range(HALVES):
                        act.wait_ge(qk_ready, b * HALVES + half + 1)
                        for dst, rows in ((q_st, slice(0, DQK)), (k_hh, slice(DQK, P))):
                            nc.scalar.activation(dst[rows, half * BANK:(half + 1) * BANK], ps[rows, half, :], ACT.Identity,
                                                 bias=bqk_sb[rows, :], scale=1.0).then_inc(qk_hi_done, 1)
                    v_hi(b, 0)
                    v_hi(b, 1)
                    v_hi(b, 2)
                    exp(b, 0)
                    for t in range(UNIT):
                        probs_hi(b, t)
                        v_hi(b, t + 3)
                        exp(b, t + 1)
                    v_hi(b, V_ITEMS - 1)
                    bc_copy(b, 0)
                    for t in range(UNIT, L1_STEPS):
                        if t < LAST:
                            exp(b, t + 1)
                        for k in SPLITS[t - UNIT]:
                            split_hi(b + 1, k)
                        probs_hi(b, t)
                    bc_copy(b, 1)

            @block.vector
            def _(dve):
                def split_lo(b, k):
                    dve.wait_ge(x_hi_done, b * KC + k + 1)
                    nc.vector.tensor_tensor(xs[1][:, k, :], x_sb[:, k % 2, :], xs[0][:, k, :].bitcast(F32),
                                            ALU.subtract).then_inc(x_lo_done, 1)

                def v_biased(b, i):
                    dve.wait_ge(v_ready, b * V_ITEMS + i + 1)
                    if i >= 3:
                        dve.wait_ge(v_lo_done, b * V_ITEMS + i - 2)
                    nc.vector.tensor_tensor(v_tmp[:, i % 3, :], ps[:, O_BANK + i % 2, :], bv_row[:],
                                            ALU.add).then_inc(v_tmp_done, 1)

                def v_lo(b, i):
                    dve.wait_ge(v_hi_done, b * V_ITEMS + i + 1)
                    nc.vector.tensor_tensor(vt[1][:, i, :], v_tmp[:, i % 3, :], vt[0][:, i, :].bitcast(F32),
                                            ALU.subtract).then_inc(v_lo_done, 1)

                def row_max(b, t):
                    dve.wait_ge(s_ready, b * L1_STEPS + t + 1)
                    nc.vector.tensor_reduce(neg_max[:, t % 4:t % 4 + 1],
                                            ps[:, S_BANK + 2 * (t % 2):S_BANK + 2 * (t % 2) + 2, :].rearrange("p a n -> p (a n)"),
                                            AX_X, ALU.max, negate=True).then_inc(max_done, 1)

                def probs_lo(b, t):
                    for j in range(2):
                        dve.wait_ge(t_hi, b * 2 * L1_STEPS + 2 * t + j + 1)
                        dst = (slice(None), t // UNIT, slice(4 * j, 4 * j + 4), slice((t % UNIT) * P, (t % UNIT + 1) * P))
                        nc.vector.tensor_tensor(pt[1][dst], ps[:, T_BANK + j, :].rearrange("p (k q) -> p k q", k=4),
                                                pt[0][dst].bitcast(F32), ALU.subtract).then_inc(t_lo, 1)

                def inverse_sums(b, unit):
                    dve.wait_ge(exp_done, b * L1_STEPS + (unit + 1) * UNIT)
                    nc.vector.reciprocal(r_inv[:], row_sum[:, unit, :]).then_inc(inv_done, 1)
                    dve.wait_ge(inv_done, b * L1_UNITS + unit + 1)
                    nc.vector.tensor_copy(r_rep[:], r_inv[:].unsqueeze(2).broadcast_to([P, UNIT, P])).then_inc(rep_done, 1)

                def output(b, j):
                    if j % KC == 0:
                        dve.wait_ge(bc_done, b * L1_UNITS + j // KC + 1)
                    dve.wait_ge(pv_ready, b * OUTS + j + 1)
                    if j >= 2:
                        dve.wait_ge(out_stored[j % 2], b * OUTS * 8 + (j // 2) * 16)
                    else:
                        dve.wait_ge(res_in[j], b * OUTS * 8 + 16)
                    nc.vector.tensor_tensor(o_sb[:, j % 2, :], ps[:, O_BANK + j % 2, :], r_bc[:, j // KC, :],
                                            ALU.mult).then_inc(o_scaled, 1)
                    if j >= 2:
                        dve.wait_ge(res_in[j % 2], b * OUTS * 8 + (j // 2) * 16 + 16)
                    dve.wait_ge(o_scaled, b * OUTS + j + 1)
                    nc.vector.scalar_tensor_tensor(o_sb[:, j % 2, :], o_sb[:, j % 2, :], gamma_sb, x_res[:, j % 2, :],
                                                   ALU.mult, ALU.add).then_inc(o_done, 1)

                dve.wait_ge(w_hi_done, 1)
                nc.vector.tensor_tensor(wqk[1][:], raw_qk, wqk[0][:].bitcast(F32), ALU.subtract).then_inc(setup_done, 1)
                for k in range(KC):
                    dve.wait_ge(x_hi_done, k + 1)
                    nc.vector.tensor_tensor(xs[1][:, k, :], first_x[:, k, :], xs[0][:, k, :].bitcast(F32),
                                            ALU.subtract).then_inc(x_lo_done, 1)
                for k in range(KC):
                    dve.wait_ge(w_hi_done, 2 + k)
                    nc.vector.tensor_tensor(wv[1][:, k, :], raw_v[:, k, :], wv[0][:, k, :].bitcast(F32),
                                            ALU.subtract).then_inc(setup_done, 1)
                dve.wait_ge(consts_in, 64)
                dve.wait_ge(setup_done, 1 + KC)
                with dve.Fori(0, B) as b:
                    for half in range(HALVES):
                        cols = slice(half * BANK, (half + 1) * BANK)
                        for n, (dst, hi, rows) in enumerate(((q_lo, q_st, slice(0, DQK)), (k_ll, k_hh, slice(DQK, P)))):
                            dve.wait_ge(qk_hi_done, b * 2 * HALVES + 2 * half + n + 1)
                            last = nc.vector.scalar_tensor_tensor(dst[rows, cols], ps[rows, half, :], bqk_sb[rows, :],
                                                                  hi[rows, cols].bitcast(F32), ALU.add, ALU.subtract)
                        last.then_inc(qk_lo_done, 1)
                    v_biased(b, 0)
                    v_biased(b, 1)
                    v_lo(b, 0)
                    v_biased(b, 2)
                    v_lo(b, 1)
                    row_max(b, 0)
                    v_lo(b, 2)
                    for t in range(UNIT):
                        v_biased(b, t + 3)
                        if t == 0:
                            row_max(b, 1)
                        probs_lo(b, t)
                        if t == UNIT - 1:
                            inverse_sums(b, 0)
                        v_lo(b, t + 3)
                        if t < UNIT - 1:
                            row_max(b, t + 2)
                    v_biased(b, V_ITEMS - 1)
                    v_lo(b, V_ITEMS - 1)
                    row_max(b, UNIT + 1)
                    for t in range(UNIT, L1_STEPS):
                        if UNIT < t < LAST:
                            row_max(b, t + 1)
                        for k in SPLITS[t - UNIT]:
                            split_lo(b + 1, k)
                        if t < LAST:
                            output(b, t - UNIT)
                        probs_lo(b, t)
                    inverse_sums(b, 1)
                    for j in range(KC - 1, OUTS):
                        output(b, j)

            @block.tensor
            def _(pe):
                THREE = ((0, 0), (0, 1), (1, 0))

                def queries_keys(b, half):
                    for k in range(KC):
                        if half == 0:
                            pe.wait_ge(x_lo_done, b * KC + k + 1)
                        for n, (w, h) in enumerate(THREE):
                            last = nc.tensor.matmul(ps[:, half, :], wqk[w][:, k, :], xs[h][:, k, half * BANK:(half + 1) * BANK],
                                                    start=(k == 0 and n == 0), stop=(k == KC - 1 and n == 2))
                    last.then_inc(qk_ready, 1)

                def values(b, i):
                    if i >= 2:
                        pe.wait_ge(v_tmp_done, b * V_ITEMS + i - 1)
                    for k in range(KC):
                        for n, (h, w) in enumerate(THREE):
                            last = nc.tensor.matmul(ps[:, O_BANK + i % 2, :], xs[h][:, k, i * P:(i + 1) * P], wv[w][:, k, :],
                                                    start=(k == 0 and n == 0), stop=(k == KC - 1 and n == 2))
                    last.then_inc(v_ready, 1)

                def scores(b, t):
                    if t >= 2:
                        pe.wait_ge(exp_done, b * L1_STEPS + t - 1)
                    for half in range(HALVES):
                        for n, k_parts in enumerate((k_hh, k_ll)):
                            last = nc.tensor.matmul(ps[:, S_BANK + 2 * (t % 2) + half, :], q_st[:, t * P:(t + 1) * P],
                                                    k_parts[:, half * BANK:(half + 1) * BANK], start=(n == 0), stop=(n == 1))
                    last.then_inc(s_ready, 1)

                def transposes(b, t):
                    pe.wait_ge(exp_done, b * L1_STEPS + t + 1)
                    if t == UNIT:
                        pe.wait_ge(bc_done, b * L1_UNITS + 1)
                    for j in range(2):
                        if t > 0:
                            pe.wait_ge(t_lo, b * 2 * L1_STEPS + 2 * (t - 1) + j + 1)
                        for k in range(4):
                            last = nc.tensor.transpose(ps[:, T_BANK + j, k * P:(k + 1) * P],
                                                       pr[:, t % 2, (4 * j + k) * P:(4 * j + k + 1) * P], ident[:])
                        last.then_inc(t_ready, 1)

                def sums_across(b, unit):
                    pe.wait_ge(rep_done, b * L1_UNITS + unit + 1)
                    pe.wait_ge(t_lo, b * 2 * L1_STEPS + 2 * UNIT * (unit + 1) - 1)
                    for q in range(UNIT):
                        last = nc.tensor.transpose(ps[:, T_BANK, q * P:(q + 1) * P], r_rep[:, q, :], ident[:])
                    last.then_inc(bc_ready, 1)

                def outputs(b, j, k_tiles):
                    unit, c = j // KC, j % KC
                    if k_tiles[0] == 0:
                        if c == 0:
                            pe.wait_ge(t_lo, b * 2 * L1_STEPS + 2 * UNIT * (unit + 1) - 1)
                        if j == 0:
                            pe.wait_ge(v_lo_done, b * V_ITEMS + V_ITEMS - 1)
                        if j >= 2:
                            pe.wait_ge(o_scaled, b * OUTS + j - 1)
                    for k in k_tiles:
                        if c == 0 and k == KT // 2:
                            pe.wait_ge(t_lo, b * 2 * L1_STEPS + 2 * UNIT * (unit + 1))
                        if j == 0 and k == KT - 1:
                            pe.wait_ge(v_lo_done, b * V_ITEMS + V_ITEMS)
                        for n, (v, p) in enumerate(THREE):
                            last = nc.tensor.matmul(ps[:, O_BANK + j % 2, :], vt[v][:, k, c * P:(c + 1) * P], pt[p][:, unit, k, :],
                                                    start=(k == 0 and n == 0), stop=(k == KT - 1 and n == 2))
                    if k_tiles[-1] == KT - 1:
                        last.then_inc(pv_ready, 1)

                pe.wait_ge(setup_done, 1)
                with pe.Fori(0, B) as b:
                    for half in range(HALVES):
                        queries_keys(b, half)
                    pe.wait_ge(setup_done, 1 + KC)
                    values(b, 0)
                    pe.wait_ge(qk_lo_done, b * HALVES + 1)
                    values(b, 1)
                    values(b, 2)
                    pe.wait_ge(consts_in, 64)
                    pe.wait_ge(stacked, b * 96 + 96)
                    scores(b, 0)
                    values(b, 3)
                    scores(b, 1)
                    for t in range(UNIT):
                        transposes(b, t)
                        if t < UNIT - 1:
                            scores(b, t + 2)
                        values(b, t + 4)
                    scores(b, UNIT + 1)
                    outputs(b, 0, range(KT // 2))
                    sums_across(b, 0)
                    outputs(b, 0, range(KT // 2, KT))
                    for t in range(UNIT, L1_STEPS):
                        if t < LAST:
                            if t > UNIT:
                                scores(b, t + 1)
                                outputs(b, t - UNIT, range(KT))
                        else:
                            outputs(b, t - UNIT, range(KT // 2))
                        transposes(b, t)
                    outputs(b, KC - 1, range(KT // 2, KT))
                    outputs(b, KC, range(KT // 2))
                    sums_across(b, 1)
                    outputs(b, KC, range(KT // 2, KT))
                    for j in range(KC + 1, OUTS):
                        outputs(b, j, range(KT))
                    pe.wait_ge(o_scaled, b * OUTS + OUTS - 1)


def build(nc, arrays):
    def dram_in(name):
        return nc.dram_tensor(name, arrays[name].shape, F32, kind="ExternalInput").ap()

    t = {name: dram_in(name) for name in arrays}
    out = nc.dram_tensor("out", (B, C, N), F32, kind="ExternalOutput").ap()
    x1 = nc.dram_tensor("x1_scratch", (B, C, N), F32, kind="Internal").ap()
    layer0(nc, t["x"], t["w_qkv"], t["w_proj"], t["gn_scale"], t["gn_bias"], t["b_qk"], t["b_v"], t["b_proj"], t["eye"], x1)
    layer1(nc, x1, t["w_qk1"], t["w_v1"], t["b_qk1"], t["b_v1"], t["gamma"], t["eye"], out)


def kernel(x, L0_conv_gn_scale, L0_conv_gn_bias, L0_conv_qkv_w, L0_conv_qkv_b, L0_conv_proj_w, L0_conv_proj_b,
           L1_conv_Wq, L1_conv_bq, L1_conv_Wk, L1_conv_bk, L1_conv_Wv, L1_conv_bv, L1_conv_gamma):
    import numpy as np
    import concourse.bacc as bacc
    from concourse.bass_utils import run_bass_kernel_spmd

    def cols(a):
        return np.ascontiguousarray(np.asarray(a).reshape(-1, P).T)

    qkv_b = np.asarray(L0_conv_qkv_b)
    arrays = {
        "x": np.ascontiguousarray(np.asarray(x).reshape(B, C, N)),
        "w_qkv": np.ascontiguousarray(np.asarray(L0_conv_qkv_w).T),
        "w_proj": np.ascontiguousarray(np.asarray(L0_conv_proj_w).T),
        "gn_scale": cols(L0_conv_gn_scale),
        "gn_bias": cols(L0_conv_gn_bias),
        "b_qk": cols(qkv_b[0:2 * C]),
        "b_v": np.ascontiguousarray(qkv_b[2 * C:3 * C].reshape(1, C)),
        "b_proj": cols(L0_conv_proj_b),
        "eye": np.eye(P, dtype=np.float32),
        "w_qk1": np.ascontiguousarray(np.concatenate([np.asarray(L1_conv_Wq), np.asarray(L1_conv_Wk)], axis=0).T),
        "w_v1": np.ascontiguousarray(np.asarray(L1_conv_Wv).T),
        "b_qk1": np.ascontiguousarray(np.concatenate([np.asarray(L1_conv_bq), np.asarray(L1_conv_bk)]).reshape(P, 1)),
        "b_v1": np.ascontiguousarray(np.asarray(L1_conv_bv).reshape(1, C)),
        "gamma": np.ascontiguousarray(np.asarray(L1_conv_gamma).reshape(1, 1)),
    }
    nc = bacc.Bacc("TRN2", target_bir_lowering=False, num_devices=1)
    build(nc, arrays)
    r = run_bass_kernel_spmd(nc, [arrays], core_ids=[0])
    return r.results[0]["out"].reshape(B, C, 32, 32)
```
